# Optimizing a Trainium2 kernel written in Bass

```python
import numpy as np
import jax
import jax.numpy as jnp

def _softmax(x, axis=-1):
    return jax.nn.softmax(x, axis=axis)

def _gelu(x):
    return jax.nn.gelu(x, approximate=True)

def _silu(x):
    return jax.nn.silu(x)

def _sigmoid(x):
    return jax.nn.sigmoid(x)

def _layernorm(x, axis=-1, eps=1e-05):
    m = jnp.mean(x, axis=axis, keepdims=True)
    v = jnp.var(x, axis=axis, keepdims=True)
    return (x - m) / jnp.sqrt(v + eps)

def _scatter_add(tgt, idx, src, axis=0):
    return tgt.at[idx].add(src)

def _segment_sum(src, seg, n):
    return jax.ops.segment_sum(src, seg, n)
kernel_name = 'mk_adj_preln_d1_adj_r2_78daf7'

def setup_inputs(seed: int=0):
    np.random.seed(seed)
    _w = jnp.asarray

    def _rec_inputs():
        import jax
        import jax.numpy as jnp
        _gk = jax.random.key(seed)
        x = -0.0002928 + 1 * jax.random.normal(jax.random.fold_in(_gk, 1), (4096, 256), jnp.float32)
        _a = jax.random.bernoulli(jax.random.fold_in(_gk, 2), 0.000488281, (4096, 4096))
        _a = jnp.logical_or(_a, jnp.swapaxes(_a, -1, -2))
        _a = jnp.logical_or(_a, jnp.eye(4096, dtype=bool))
        adj = _a.astype(jnp.int32)
        return (x, adj)
    x, adj = _rec_inputs()

    def _L0_gnn_setup():
        import jax, jax.numpy as jnp
        import numpy as np
        N_X, N_NEIGH, D_IN, D_HID, D_OUT = (4096, 4096, 256, 32, 128)
        NEG_BIG = -9000000000000000.0
        key = jax.random.key(seed)
        ks = jax.random.split(key, 16)
        s_in = 1.0 / np.sqrt(D_IN)
        s_hid = 1.0 / np.sqrt(D_HID)
        return {'x': jax.random.normal(ks[0], (N_X, D_IN), jnp.float32), 'neigh': jax.random.normal(ks[1], (N_NEIGH, D_IN), jnp.float32), 'adj': jax.random.randint(ks[2], (N_X, N_NEIGH), 0, 2, jnp.int32), 'Wx1': jax.random.uniform(ks[3], (D_IN, D_HID), jnp.float32, -s_in, s_in), 'bx1': jnp.zeros((D_HID,), jnp.float32), 'Wx2': jax.random.uniform(ks[4], (D_HID, D_HID), jnp.float32, -s_hid, s_hid), 'bx2': jnp.zeros((D_HID,), jnp.float32), 'Wn1': jax.random.uniform(ks[5], (D_IN, D_HID), jnp.float32, -s_in, s_in), 'bn1': jnp.zeros((D_HID,), jnp.float32), 'Wn2': jax.random.uniform(ks[6], (D_HID, D_HID), jnp.float32, -s_hid, s_hid), 'bn2': jnp.zeros((D_HID,), jnp.float32), 'Wv': jax.random.uniform(ks[7], (D_IN, D_OUT), jnp.float32, -s_in, s_in), 'bv': jnp.zeros((D_OUT,), jnp.float32), 'Wfx': jax.random.uniform(ks[8], (D_IN, D_OUT), jnp.float32, -s_in, s_in), 'bfx': jnp.zeros((D_OUT,), jnp.float32)}
    _L0_gnn_all = _L0_gnn_setup()
    _L0_gnn_in = {k: v for k, v in _L0_gnn_all.items() if k in ('neigh', 'Wx1', 'bx1', 'Wx2', 'bx2', 'Wn1', 'bn1', 'Wn2', 'bn2', 'Wv', 'bv', 'Wfx', 'bfx')}
    del _L0_gnn_all
    return {'x': x, 'adj': adj, 'L0_gnn_neigh': _L0_gnn_in['neigh'], 'L0_gnn_Wx1': _L0_gnn_in['Wx1'], 'L0_gnn_bx1': _L0_gnn_in['bx1'], 'L0_gnn_Wx2': _L0_gnn_in['Wx2'], 'L0_gnn_bx2': _L0_gnn_in['bx2'], 'L0_gnn_Wn1': _L0_gnn_in['Wn1'], 'L0_gnn_bn1': _L0_gnn_in['bn1'], 'L0_gnn_Wn2': _L0_gnn_in['Wn2'], 'L0_gnn_bn2': _L0_gnn_in['bn2'], 'L0_gnn_Wv': _L0_gnn_in['Wv'], 'L0_gnn_bv': _L0_gnn_in['bv'], 'L0_gnn_Wfx': _L0_gnn_in['Wfx'], 'L0_gnn_bfx': _L0_gnn_in['bfx']}

def reference(x, adj, L0_gnn_neigh, L0_gnn_Wx1, L0_gnn_bx1, L0_gnn_Wx2, L0_gnn_bx2, L0_gnn_Wn1, L0_gnn_bn1, L0_gnn_Wn2, L0_gnn_bn2, L0_gnn_Wv, L0_gnn_bv, L0_gnn_Wfx, L0_gnn_bfx):
    import jax
    import jax.numpy as jnp

    def _L0_gnn_ref(x, neigh, adj, Wx1, bx1, Wx2, bx2, Wn1, bn1, Wn2, bn2, Wv, bv, Wfx, bfx):
        import jax, jax.numpy as jnp
        import numpy as np
        N_X, N_NEIGH, D_IN, D_HID, D_OUT = (4096, 4096, 256, 32, 128)
        NEG_BIG = -9000000000000000.0
        neib_att = jnp.tanh(neigh @ Wn1 + bn1) @ Wn2 + bn2
        value = neigh @ Wv + bv
        x_att = jnp.tanh(x @ Wx1 + bx1) @ Wx2 + bx2
        ws = jnp.einsum('nh,mh->nm', x_att, neib_att)
        ws = jax.nn.leaky_relu(ws, negative_slope=0.01)
        ws = jnp.where(adj > 0, ws, jnp.float32(NEG_BIG))
        ws = jax.nn.softmax(ws, axis=1)
        agg_neib = ws @ value
        out = jnp.concatenate([x @ Wfx + bfx, agg_neib], axis=1)
        return out
    h = jnp.maximum(_layernorm(x, axis=-1), 0.0)
    x = x + _L0_gnn_ref(h, L0_gnn_neigh, adj, L0_gnn_Wx1, L0_gnn_bx1, L0_gnn_Wx2, L0_gnn_bx2, L0_gnn_Wn1, L0_gnn_bn1, L0_gnn_Wn2, L0_gnn_bn2, L0_gnn_Wv, L0_gnn_bv, L0_gnn_Wfx, L0_gnn_bfx)
    return x

_drawn_inputs = setup_inputs


def setup_inputs(seed=0):
    import zlib

    import numpy as np

    out = dict(_drawn_inputs(seed))
    spreads = {'L0_gnn_bx1': (0.0, 2.0),
     'L0_gnn_bx2': (0.0, 0.585),
     'L0_gnn_bn1': (0.0, 2.0),
     'L0_gnn_bn2': (0.0, 2.0),
     'L0_gnn_bv': (0.0, 0.1),
     'L0_gnn_bfx': (0.0, 0.1)}
    factors = {'L0_gnn_Wx1': 8.0, 'L0_gnn_Wx2': 8.0, 'L0_gnn_Wn1': 8.0, 'L0_gnn_Wn2': 8.0}
    for name, (base, spread) in spreads.items():
        noise = np.random.default_rng([zlib.crc32(name.encode()), seed]).standard_normal(out[name].shape)
        drawn = base * np.exp(spread * noise) if base else spread * noise
        out[name] = jnp.asarray(drawn.astype(out[name].dtype))
    for name, factor in factors.items():
        out[name] = (out[name] * factor).astype(out[name].dtype)
    return out
```

```python
from contextlib import ExitStack

import concourse.bass as bass
from concourse import mybir

FP32 = mybir.dt.float32
FP32R = mybir.dt.float32r
BF16 = mybir.dt.bfloat16
INT32 = mybir.dt.int32
ALU = mybir.AluOpType
ACT = mybir.ActivationFunctionType
AX = mybir.AxisListType

P = 128
N_X, N_NEIGH, D_IN, D_HID, D_OUT = 4096, 4096, 256, 32, 128
KT = D_IN // P
BANK = 512
GROUP = BANK
TILES = GROUP // P
GROUPS = N_X // GROUP
NEIGH_GROUPS = N_NEIGH // GROUP
CHUNK = 2 * BANK
CHUNKS = N_NEIGH // CHUNK
STEPS = GROUPS * TILES * CHUNKS
GSTEPS = TILES * CHUNKS
BLOCKS = N_NEIGH // P
PERIOD = 2 * GSTEPS
EPS = 1e-5
MASKED = -float(2 ** 53)
SLOPE = 0.01
RISE = 99.0

ADJ_RING = 4
CONSTS_IN = 16 * 2 * (5 + P // D_HID)
EXP_LAG = CHUNKS + 1
BACK_LAG = GSTEPS + 2
COPY_LAG = BACK_LAG + GSTEPS
FIN_LAG = COPY_LAG + 2
SUM_LAG = GSTEPS + EXP_LAG + 1
LOOP_START, LOOPS = SUM_LAG + 1, 2
END = STEPS + FIN_LAG - GSTEPS + 2


def build(nc, x, adj, neigh, wx1, bx1, wx2, bx2, wn1, bn1, wn2, bn2, wv, bv, wfx, bfx, out):
    assert LOOP_START + LOOPS * PERIOD <= STEPS - ADJ_RING
    assert LOOP_START >= BACK_LAG
    with ExitStack() as ctx:
        def sb(name, shape, dt):
            return ctx.enter_context(nc.sbuf_tensor(name, shape, dt))

        def sem(name):
            return ctx.enter_context(nc.semaphore(name))

        scores = sb("scores", [P, 2 * TILES, N_NEIGH], FP32)
        neib = sb("neib", [P, N_NEIGH], FP32R)
        v_hi = sb("v_hi", [P, BLOCKS, D_OUT], FP32R)
        v_lo = sb("v_lo", [P, BLOCKS, D_OUT], FP32R)
        adj_in = sb("adj_in", [P, ADJ_RING, CHUNK], INT32)
        mask = sb("mask", [P, 2, CHUNK], BF16)
        xs = sb("xs", [P, 2, GROUP], FP32R)
        pt_hi = sb("pt_hi", [P, 2, GROUP], FP32R)
        pt_lo = sb("pt_lo", [P, 2, GROUP], FP32R)
        agg = sb("agg", [P, GROUP], FP32)
        x_right = sb("x_right", [P, TILES, D_OUT], FP32)
        out_right = sb("out_right", [P, TILES, D_OUT], FP32)
        ident = sb("ident", [P, P], FP32)
        diag = sb("diag", [P, P], BF16)
        top = sb("top", [P, 2, CHUNKS], FP32)
        neg_top = sb("neg_top", [P, 2, 1], FP32)
        sums = sb("sums", [P, 2, TILES, CHUNKS], FP32)
        row_sum = sb("row_sum", [P, TILES], FP32)
        inv_sum = sb("inv_sum", [P, 2, TILES], FP32)
        w1 = sb("w1", [P, 2, KT, D_HID], FP32)
        w2 = sb("w2", [D_HID, 2, P], FP32)
        b1 = sb("b1", [D_HID, 2], FP32)
        b2 = sb("b2", [P, 2], FP32)
        stats = sb("stats", [P, 2, TILES, 6], FP32)
        new_mean_var = sb("new_mean_var", [P, 2, TILES, 2], FP32)
        mean_var = sb("mean_var", [P, GROUPS * TILES, 2], FP32)
        rstd = sb("rstd", [P, GROUPS * TILES], FP32)
        eps = sb("eps", [P, 1], FP32)

        def scratch(buffer, start, *shape):
            n = 1
            for s in shape:
                n *= s
            ap = scores[:, buffer, start:start + n]
            names = " ".join(f"d{i}" for i in range(len(shape)))
            sizes = {f"d{i}": s for i, s in enumerate(shape)}
            return ap.rearrange(f"p ({names}) -> p {names}", **sizes)

        x_all = scores[:, 0:2, :].rearrange("p a (t d) -> p (a t) d", d=D_IN)
        rows = scratch(2, 0, 2, TILES, D_IN)
        rows_t = scratch(2, 2048, 2, KT * GROUP)
        hidden = scratch(3, 0, 2, GROUP)
        value = scratch(3, 1024, TILES * D_OUT)
        x_left = scratch(3, 1536, 2, TILES * D_OUT)
        out_left = scratch(3, 2560, 2, TILES * D_OUT)
        w_wide = scratch(4, 0, 2, KT, D_OUT)
        b_wide = scratch(4, 1024, 2, TILES * D_OUT)

        ps = ctx.enter_context(nc.psum_tensor("ps_scores", [P, 2, CHUNK], FP32))
        pt = ctx.enter_context(nc.psum_tensor("ps_turned", [P, 2, BANK], FP32))
        pa = ctx.enter_context(nc.psum_tensor("ps_product", [P, 2, BANK], FP32))
        ps_value, ps_hidden, ps_att = ps[:, 0, 0:BANK], pa[0:D_HID, 0, :], pa[:, 1, :]

        xs_dram = nc.dram_tensor("xs_scratch", (GROUPS, P, GROUP), FP32, kind="Internal").ap()

        consts_in, x_in = sem("consts_in"), sem("x_in")
        rows_in = [sem("rows_in0"), sem("rows_in1")]
        made = sem("made")
        fills = sem("fills")
        rows_ready = sem("rows_ready")
        turned = sem("turned")
        turned_out = sem("turned_out")
        first_done = sem("first_done")
        hidden_done = sem("hidden_done")
        wide_done = sem("wide_done")
        wide_out = sem("wide_out")
        second_done = sem("second_done")
        att_out = sem("att_out")
        att_hi = sem("att_hi")
        v_hi_done, v_lo_done = sem("v_hi_done"), sem("v_lo_done")
        stats_done, aggr_done, kept = sem("stats_done"), sem("aggr_done"), sem("kept")
        joined = sem("joined")
        std_done, rstd_done = sem("std_done"), sem("rstd_done")
        x_left_done = sem("x_left_done")
        left_out = [sem("left_out0"), sem("left_out1")]
        xs_out = [sem("xs_out0"), sem("xs_out1")]
        adj_ready = [sem(f"adj_ready{i}") for i in range(ADJ_RING)]
        xs_ready = [sem("xs_ready0"), sem("xs_ready1")]
        mask_done = sem("mask_done")
        scored = sem("scored")
        risen = sem("risen")
        leaked = sem("leaked")
        top_done = sem("top_done")
        exp_done = sem("exp_done")
        block_turned = sem("block_turned")
        hi_done, lo_done = sem("hi_done"), sem("lo_done")
        block_used = sem("block_used")
        agg_out = sem("agg_out")
        agg_turned = sem("agg_turned")
        row_sum_done, sums_done = sem("row_sum_done"), sem("sums_done")
        right_done = sem("right_done")
        x_right_in = sem("x_right_in")
        right_out = sem("right_out")

        block = ctx.enter_context(nc.Block())

        def encode(engine, step):
            for e in range(2):
                step(e, 0)
            with engine.Fori(1, GROUPS // 2 - 1) as it:
                for e in range(2):
                    step(e, it)
            for e in range(GROUPS - 2, GROUPS):
                step(e, 0)

        def wait(engine, semaphore, value):
            if not isinstance(value, int) or value > 0:
                engine.wait_ge(semaphore, value)

        def main(engine, step):
            for s in range(LOOP_START):
                step(s, 0)
            with engine.Fori(0, LOOPS) as it:
                for s in range(LOOP_START, LOOP_START + PERIOD):
                    step(s, it)
            for s in range(LOOP_START + LOOPS * PERIOD, END):
                step(s, 0)

        def chunk_of(s):
            return s // GSTEPS % 2, s // CHUNKS % TILES, s % CHUNKS

        @block.sync
        def _(sp):
            for i in range(ADJ_RING):
                sp.dma_start(adj_in[:, i, :], adj[0:P, i * CHUNK:(i + 1) * CHUNK]).then_inc(adj_ready[i], 16)
            x_tiles = x.rearrange("(t p) d -> p t d", p=P)
            neigh_tiles = neigh.rearrange("(t p) d -> p t d", p=P)
            out_tiles = out.rearrange("(t p) d -> p t d", p=P)

            def load_neigh(par, it):
                e = 2 * it + par
                sp.dma_start(rows[:, par % 2], neigh_tiles[:, bass.ds(e * TILES, TILES), :]).then_inc(
                    rows_in[par % 2], 16)

            load_neigh(0, 0)
            load_neigh(1, 0)
            for g in range(4):
                sp.dma_start(x_all[:, 8 * g:8 * g + 8, :], x_tiles[:, 8 * g:8 * g + 8, :]).then_inc(x_in, 16)
            with sp.Fori(1, NEIGH_GROUPS // 2) as it:
                for par in range(2):
                    sp.wait_ge(turned, 2 * it + par - 1)
                    load_neigh(par, it)

            def store_left(par, it):
                e = 2 * it + par
                sp.wait_ge(wide_out, NEIGH_GROUPS + e + 1)
                sp.dma_start(out_tiles[:, bass.ds(e * TILES, TILES), 0:D_OUT],
                             out_left[:, par].rearrange("p (t d) -> p t d", d=D_OUT)).then_inc(left_out[par], 16)
                sp.wait_ge(att_out, NEIGH_GROUPS + e + 1)
                sp.dma_start(xs_dram[bass.ds(e, 1)].rearrange("a p n -> p (a n)"), xs[:, par, :].bitcast(FP32)).then_inc(
                    xs_out[par], 16)

            with sp.Fori(0, GROUPS // 2) as it:
                for par in range(2):
                    store_left(par, it)
            for par in range(2):
                sp.wait_ge(xs_out[par], 16 * GROUPS // 2)

            def load_xs(par, g):
                sp.dma_start(xs[:, par, :].bitcast(FP32), xs_dram[bass.ds(g, 1)].rearrange("a p n -> p (a n)")).then_inc(
                    xs_ready[par], 16)

            def load_x_right(g):
                sp.dma_start(x_right[:, :, :],
                             x_tiles[:, bass.ds(g * TILES, TILES), D_OUT:2 * D_OUT]).then_inc(x_right_in, 16)

            load_xs(0, 0)
            load_xs(1, 1)
            load_x_right(0)

            def step(s, it):
                k = s + PERIOD * it
                if s + ADJ_RING < STEPS:
                    _, _, c = chunk_of(s)
                    n = s + ADJ_RING
                    tile = n // CHUNKS + 2 * TILES * it
                    sp.wait_ge(mask_done, k + 1)
                    sp.dma_start(adj_in[:, n % ADJ_RING, :],
                                 adj[bass.ds(tile * P, P), n % CHUNKS * CHUNK:(n % CHUNKS + 1) * CHUNK]).then_inc(
                        adj_ready[n % ADJ_RING], 16)
                if s % GSTEPS == GSTEPS - 4 and GSTEPS <= s < STEPS - GSTEPS:
                    g = s // GSTEPS + 2 * it
                    sp.wait_ge(scored, (g * GSTEPS))
                    load_xs((s // GSTEPS + 1) % 2, g + 1)
                if (s - FIN_LAG - 2) % GSTEPS == 0 and s >= FIN_LAG + 2:
                    g0 = (s - FIN_LAG - 2) // GSTEPS
                    g = g0 + 2 * it
                    sp.wait_ge(right_done, g + 1)
                    sp.dma_start(out_tiles[:, bass.ds(g * TILES, TILES), D_OUT:2 * D_OUT],
                                 out_right[:, :, :]).then_inc(right_out, 16)
                    if g0 < GROUPS - 1:
                        load_x_right(g + 1)

            main(sp, step)
            sp.wait_ge(right_done, GROUPS)
            sp.dma_start(out_tiles[:, (GROUPS - 1) * TILES:GROUPS * TILES, D_OUT:2 * D_OUT],
                         out_right[:, :, :]).then_inc(right_out, 16)
            for par in range(2):
                sp.wait_ge(left_out[par], 16 * GROUPS // 2)
            sp.wait_ge(right_out, 16 * GROUPS)

        @block.gpsimd
        def _(pool):
            pool.memset(ident[:, :], 0.0).then_inc(fills, 1)
            pool.memset(diag[:, :], 0.0).then_inc(fills, 1)
            pool.memset(eps[:, :], EPS).then_inc(made, 1)
            pool.wait_ge(fills, 2)
            pool.affine_select(out=ident[:, :], in_=ident[:, :], compare_op=ALU.not_equal, fill=1.0,
                               base=0, pattern=[[-1, P]], channel_multiplier=1).then_inc(made, 1)
            pool.affine_select(out=diag[:, :], in_=diag[:, :], compare_op=ALU.not_equal, fill=MASKED,
                               base=0, pattern=[[-1, P]], channel_multiplier=1).then_inc(made, 1)
            pool.wait_ge(consts_in, CONSTS_IN)
            pool.wait_ge(x_in, 16 * 4)
            with pool.Fori(0, GROUPS // 2) as it:
                for par in range(2):
                    e = 2 * it + par
                    pool.wait_ge(wide_out, NEIGH_GROUPS - 1 + e)
                    pool.tensor_tensor(
                        x_left[:, par].rearrange("p (t d) -> p t d", d=D_OUT),
                        x_all[:, bass.ds(e * TILES, TILES), 0:D_OUT],
                        b_wide[:, 1].rearrange("p (t d) -> p t d", d=D_OUT), ALU.add).then_inc(x_left_done, 1)

        @block.scalar
        def _(act):
            for side, (w, b, v, c, ww, bw) in enumerate(((wn1, bn1, wn2, bn2, wv, bv), (wx1, bx1, wx2, bx2, wfx, bfx))):
                act.dma_start(w1[:, side], w.rearrange("(k p) h -> p k h", p=P)).then_inc(consts_in, 16)
                act.dma_start(w_wide[:, side], ww.rearrange("(k p) d -> p k d", p=P)).then_inc(consts_in, 16)
                act.dma_start(b1[:, side:side + 1], b.rearrange("(p a) -> p a", a=1)).then_inc(consts_in, 16)
                act.dma_start(b_wide[:, side].rearrange("p (t d) -> p t d", d=D_OUT),
                              bw.rearrange("(a t d) -> a t d", a=1, t=1).to_broadcast([P, TILES, D_OUT])).then_inc(
                    consts_in, 16)
                act.dma_start(w2[:, side].rearrange("p (r h) -> p r h", h=D_HID),
                              v.rearrange("p (a h) -> p a h", a=1).to_broadcast([D_HID, P // D_HID, D_HID])).then_inc(
                    consts_in, 16)
                for r in range(P // D_HID):
                    act.dma_start(b2[r * D_HID:(r + 1) * D_HID, side:side + 1],
                                  c.rearrange("(p a) -> p a", a=1)).then_inc(consts_in, 16)

            def turned_copy(side, q, par):
                act.wait_ge(turned, q + 1)
                wait(act, wide_done, q - 1)
                act.activation(rows_t[:, par], pt[:, :, :].rearrange("p a n -> p (a n)"),
                               ACT.Relu if side else ACT.Copy).then_inc(turned_out, 1)

            def encode_step(side, e, it):
                q = side * NEIGH_GROUPS + e + 2 * it
                par = e % 2
                act.wait_ge(first_done, q + 1)
                wait(act, second_done, q - 1)
                act.activation(hidden[0:D_HID, par], ps_hidden, ACT.Tanh, bias=b1[:, side:side + 1]).then_inc(
                    hidden_done, 1)
                if e < 7:
                    turned_copy(side, q + 1, 1 - par)

            act.wait_ge(consts_in, CONSTS_IN)
            for side in range(2):
                if side:
                    act.wait_ge(kept, GROUPS)
                    act.activation(rstd[:, :], mean_var[:, :, 1], ACT.Sqrt, bias=eps[:, :]).then_inc(std_done, 1)
                turned_copy(side, side * NEIGH_GROUPS, 0)
                encode(act, lambda e, it: encode_step(side, e, it))
            act.wait_ge(second_done, 2 * GROUPS)
            act.wait_ge(v_lo_done, NEIGH_GROUPS)
            act.wait_ge(wide_out, 2 * GROUPS)
            act.wait_ge(att_out, 2 * GROUPS)
            for par in range(2):
                act.wait_ge(left_out[par], 16 * GROUPS // 2)

            def hi(s, u, it):
                b = s - BACK_LAG
                if not 0 <= b < STEPS:
                    return
                j = 2 * b + u + 2 * PERIOD * it
                act.wait_ge(block_turned, j + 1)
                if 2 * b + u >= 2:
                    act.wait_ge(block_used, j - 1)
                act.activation(pt_hi[:, u], pt[:, u], ACT.Copy).then_inc(hi_done, 1)

            def step(s, it):
                k = s + PERIOD * it
                hi(s, 0, it)
                e = s - EXP_LAG
                if 0 <= e < STEPS:
                    parity, tile, c = chunk_of(e)
                    t = e // CHUNKS + 2 * TILES * it
                    if c == 0:
                        act.wait_ge(top_done, t + 1)
                        if tile == 0 and e >= 2 * GSTEPS:
                            act.wait_ge(sums_done, e // GSTEPS - 1 + 2 * it)
                    cols = scores[:, parity * TILES + tile, c * CHUNK:(c + 1) * CHUNK]
                    act.activation(cols, cols, ACT.Exp, bias=neg_top[:, tile % 2, :],
                                   accum_out=sums[:, parity, tile, c:c + 1]).then_inc(exp_done, 1)
                hi(s, 1, it)
                if s < STEPS:
                    parity, tile, c = chunk_of(s)
                    act.wait_ge(scored, k + 1)
                    if tile == 0 and s >= 2 * GSTEPS:
                        act.wait_ge(block_turned, (s // GSTEPS - 2) * BLOCKS + (c + 1) * BLOCKS // CHUNKS + 2 * BLOCKS * it)
                    act.activation(scores[:, parity * TILES + tile, c * CHUNK:(c + 1) * CHUNK], ps[:, s % 2],
                                   ACT.Relu, scale=RISE).then_inc(risen, 1)
                b = s - COPY_LAG
                if b >= 0 and b % GSTEPS == 0 and b // GSTEPS < GROUPS:
                    g = b // GSTEPS + 2 * it
                    act.wait_ge(block_used, (g + 1) * BLOCKS)
                    if b:
                        act.wait_ge(agg_turned, g)
                    act.activation(agg[:, :], pa[:, b // GSTEPS % 2], ACT.Copy).then_inc(agg_out, 1)

            main(act, step)

        @block.vector
        def _(dve):
            def stats_of(e, it):
                t0 = (e + 2 * it) * TILES
                dve.wait_ge(x_in, 16 * 4)
                wait(dve, aggr_done, e + 2 * it - 1)
                for i in range(TILES):
                    last = dve.bn_stats(stats[:, e % 2, i, :],
                                        x_all[:, bass.ds(t0 + i, 1), :].rearrange("p a b -> p (a b)"))
                last.then_inc(stats_done, 1)

            def aggr_of(e):
                for i in range(TILES):
                    last = dve.bn_aggr(new_mean_var[:, e % 2, i, :], stats[:, e % 2, i, :])
                last.then_inc(aggr_done, 1)

            def keep_aggr(e, it):
                dve.wait_ge(aggr_done, e + 2 * it + 1)
                dve.tensor_copy(mean_var[:, bass.ds((e + 2 * it) * TILES, TILES), :],
                                new_mean_var[:, e % 2]).then_inc(kept, 1)

            def neigh_step(e, it):
                q = e + 2 * it
                par = e % 2
                dve.wait_ge(wide_done, q + 1)
                wait(dve, v_lo_done, q)
                dve.tensor_tensor(value, ps_value, b_wide[:, 0], ALU.add).then_inc(wide_out, 1)
                stats_of(e, it)
                dve.wait_ge(wide_out, q + 1)
                hi = v_hi[:, bass.ds(q * TILES, TILES), :].rearrange("p t d -> p (t d)")
                lo = v_lo[:, bass.ds(q * TILES, TILES), :].rearrange("p t d -> p (t d)")
                dve.tensor_copy(hi, value).then_inc(v_hi_done, 1)
                dve.wait_ge(stats_done, q + 1)
                wait(dve, kept, q - 1)
                dve.sem_inc(joined, 1)
                aggr_of(e)
                dve.wait_ge(v_hi_done, q + 1)
                dve.tensor_tensor(lo, value, hi.bitcast(FP32), ALU.subtract).then_inc(v_lo_done, 1)
                keep_aggr(e, it)
                dve.wait_ge(second_done, q + 1)
                cols = neib[:, bass.ds(q * GROUP, GROUP)]
                dve.tensor_scalar(cols, ps_att, b2[:, 0:1], None, ALU.add).then_inc(att_hi, 1)
                dve.wait_ge(att_hi, q + 1)
                for p in (D_HID, 3 * D_HID):
                    part = neib[p:p + D_HID, bass.ds(q * GROUP, GROUP)]
                    last = dve.scalar_tensor_tensor(part, pa[p:p + D_HID, 1, :], b2[p:p + D_HID, 0:1],
                                                    part.bitcast(FP32), ALU.add, ALU.subtract)
                last.then_inc(att_out, 1)

            def normalise(e, it):
                t0 = (e + 2 * it) * TILES
                par = e % 2
                dve.wait_ge(turned, NEIGH_GROUPS + e + 2 * it - 1)
                for i in range(TILES):
                    last = dve.tensor_scalar(
                        rows[:, par, i, :], x_all[:, bass.ds(t0 + i, 1), :].rearrange("p a b -> p (a b)"),
                        mean_var[:, bass.ds(t0 + i, 1), 0:1].rearrange("p a b -> p (a b)"),
                        rstd[:, bass.ds(t0 + i, 1)], ALU.subtract, ALU.mult)
                last.then_inc(rows_ready, 1)

            def x_step(e, it):
                n = e + 2 * it
                q = NEIGH_GROUPS + n
                par = e % 2
                if e < 7:
                    normalise(e + 1, it)
                dve.wait_ge(wide_done, q + 1)
                dve.wait_ge(x_left_done, n + 1)
                wait(dve, left_out[par], 16 * (e // 2 + it))
                dve.tensor_tensor(out_left[:, par], ps_value, x_left[:, par], ALU.add).then_inc(wide_out, 1)
                dve.wait_ge(second_done, q + 1)
                wait(dve, xs_out[par], 16 * (e // 2 + it))
                dve.tensor_scalar(xs[:, par, :], ps_att, b2[:, 1:2], None, ALU.add).then_inc(att_hi, 1)
                dve.wait_ge(att_hi, q + 1)
                low = xs[P // 2:P, par, :]
                dve.scalar_tensor_tensor(low, pa[P // 2:P, 1, :], b2[P // 2:P, 1:2], low.bitcast(FP32),
                                         ALU.add, ALU.subtract).then_inc(att_out, 1)

            dve.wait_ge(consts_in, CONSTS_IN)
            encode(dve, neigh_step)
            dve.wait_ge(std_done, 1)
            dve.reciprocal(rstd[:, :], rstd[:, :]).then_inc(rstd_done, 1)
            dve.wait_ge(rstd_done, 1)
            normalise(0, 0)
            encode(dve, x_step)

            def mask_of(n, it):
                k = n + PERIOD * it
                dve.wait_ge(adj_ready[n % ADJ_RING], 16 * (n // ADJ_RING + 1) + 16 * PERIOD // ADJ_RING * it)
                if n >= 2:
                    dve.wait_ge(scored, k - 1)
                dve.tensor_scalar(mask[:, n % 2, :], adj_in[:, n % ADJ_RING, :], 0.0, None, ALU.is_le).then_inc(
                    mask_done, 1)

            def lo(s, u, it):
                b = s - BACK_LAG
                if not 0 <= b < STEPS:
                    return
                j = 2 * b + u + 2 * PERIOD * it
                dve.wait_ge(hi_done, j + 1)
                dve.tensor_tensor(pt_lo[:, u], pt[:, u], pt_hi[:, u].bitcast(FP32), ALU.subtract).then_inc(
                    lo_done, 1)

            def step(s, it):
                n = s - 1
                if 0 <= n < STEPS:
                    parity, tile, c = chunk_of(n)
                    k = n + PERIOD * it
                    cols = scores[:, parity * TILES + tile, c * CHUNK:(c + 1) * CHUNK]
                    dve.wait_ge(risen, k + 1)
                    if c:
                        dve.wait_ge(leaked, k)
                    start = top[:, tile % 2, c - 1:c] if c else -3.0e38
                    if c == 0 and n >= 2 * CHUNKS:
                        dve.wait_ge(top_done, n // CHUNKS - 1 + 2 * TILES * it)
                    dve.sem_inc(joined, 1)
                    dve.tensor_tensor_reduce(cols, ps[:, n % 2], cols, SLOPE, start, ALU.add, ALU.max,
                                             top[:, tile % 2, c:c + 1]).then_inc(leaked, 1)
                lo(s, 0, it)
                if 0 <= n < STEPS and n % CHUNKS == CHUNKS - 1:
                    dve.wait_ge(leaked, n + 1 + PERIOD * it)
                    if n >= 2 * CHUNKS:
                        dve.wait_ge(exp_done, (n // CHUNKS - 1) * CHUNKS + PERIOD * it)
                    dve.tensor_scalar(neg_top[:, n // CHUNKS % 2, :], top[:, n // CHUNKS % 2, CHUNKS - 1:CHUNKS],
                                      -1.0, None, ALU.mult).then_inc(top_done, 1)
                if s + 1 < STEPS:
                    mask_of(s + 1, it)
                lo(s, 1, it)
                b = s - SUM_LAG
                if b >= 0 and b % GSTEPS == 0 and b // GSTEPS < GROUPS:
                    g = b // GSTEPS + 2 * it
                    parity = b // GSTEPS % 2
                    dve.wait_ge(exp_done, (g + 1) * GSTEPS)
                    if b:
                        dve.wait_ge(sums_done, g)
                    dve.reduce_sum(row_sum[:, :], sums[:, parity], axis=AX.X).then_inc(row_sum_done, 1)
                    dve.wait_ge(row_sum_done, g + 1)
                    if b:
                        dve.wait_ge(right_done, g)
                    dve.reciprocal(inv_sum[:, parity, :], row_sum[:, :]).then_inc(sums_done, 1)
                b = s - FIN_LAG
                if b >= 0 and b % GSTEPS == 0 and b // GSTEPS < GROUPS:
                    g = b // GSTEPS + 2 * it
                    parity = b // GSTEPS % 2
                    dve.wait_ge(agg_turned, g + 1)
                    dve.wait_ge(sums_done, g + 1)
                    dve.wait_ge(x_right_in, 16 * (g + 1))
                    if b:
                        dve.wait_ge(right_out, 16 * g)
                    for i in range(TILES):
                        last = dve.scalar_tensor_tensor(
                            out_right[:, i, :], pa[:, parity, i * P:(i + 1) * P], inv_sum[:, parity, i:i + 1],
                            x_right[:, i, :], ALU.mult, ALU.add)
                    last.then_inc(right_done, 1)

            mask_of(0, 0)
            main(dve, step)

        @block.tensor
        def _(pe):
            def turn_rows(side, q, e, it):
                par = e % 2
                if side:
                    pe.wait_ge(rows_ready, e + 2 * it + 1)
                else:
                    pe.wait_ge(rows_in[par], 16 * (e // 2 + it + 1))
                wait(pe, turned_out, q)
                for k in range(KT):
                    for i in range(TILES):
                        last = pe.transpose(pt[:, k, i * P:(i + 1) * P], rows[:, par, i, k * P:(k + 1) * P],
                                            ident[:, :])
                last.then_inc(turned, 1)

            def encode_step(side, e, it):
                q = side * NEIGH_GROUPS + e + 2 * it
                par = e % 2
                pe.wait_ge(turned_out, q + 1)
                wait(pe, hidden_done, q)
                for k in range(KT):
                    last = pe.matmul(ps_hidden, w1[:, side, k, :], rows_t[:, par, k * GROUP:(k + 1) * GROUP],
                                     start=k == 0, stop=k == KT - 1)
                last.then_inc(first_done, 1)
                wait(pe, wide_out, q)
                for i in range(TILES):
                    for k in range(KT):
                        last = pe.matmul(ps[:, 0, i * D_OUT:(i + 1) * D_OUT],
                                         rows_t[:, par, k * GROUP + i * P:k * GROUP + (i + 1) * P],
                                         w_wide[:, side, k, :], start=k == 0, stop=k == KT - 1)
                last.then_inc(wide_done, 1)
                if e < 7:
                    turn_rows(side, q + 1, e + 1, it)
                pe.wait_ge(hidden_done, q + 1)
                wait(pe, att_out, q)
                pe.matmul(ps_att, w2[:, side, :], hidden[0:D_HID, par], start=True, stop=True).then_inc(
                    second_done, 1)

            pe.wait_ge(made, 3)
            pe.wait_ge(consts_in, CONSTS_IN)
            for side in range(2):
                turn_rows(side, side * NEIGH_GROUPS, 0, 0)
                encode(pe, lambda e, it: encode_step(side, e, it))
            pe.wait_ge(wide_out, 2 * GROUPS)
            pe.wait_ge(att_out, 2 * GROUPS)

            def score(s, h, it):
                if s >= STEPS:
                    return
                k = s + PERIOD * it
                parity, tile, c = chunk_of(s)
                if h == 0:
                    pe.wait_ge(mask_done, k + 1)
                    if s >= 2:
                        pe.wait_ge(leaked, k - 1)
                    if tile == 0 and c == 0:
                        pe.wait_ge(xs_ready[parity], 16 * (s // PERIOD + 1 + it))
                half = slice(h * BANK, (h + 1) * BANK)
                pe.matmul(ps[:, s % 2, half], diag[:, :], mask[:, s % 2, half], start=True, stop=False)
                last = pe.matmul(ps[:, s % 2, half], xs[:, parity, tile * P:(tile + 1) * P],
                                 neib[:, c * CHUNK + h * BANK:c * CHUNK + (h + 1) * BANK], start=False, stop=True)
                if h == 1:
                    last.then_inc(scored, 1)

            def turn(s, u, it):
                b = s - BACK_LAG
                if not 0 <= b < STEPS:
                    return
                parity = b // GSTEPS % 2
                n = 2 * (b % GSTEPS) + u
                j = 2 * b + u + 2 * PERIOD * it
                per_chunk = BLOCKS // CHUNKS
                if n % per_chunk == 0:
                    pe.wait_ge(exp_done, (b // GSTEPS + 1) * GSTEPS - CHUNKS + n // per_chunk + 1 + PERIOD * it)
                if 2 * b + u >= 2:
                    pe.wait_ge(lo_done, j - 1)
                for i in range(TILES):
                    last = pe.transpose(pt[:, u, i * P:(i + 1) * P],
                                        scores[:, parity * TILES + i, n * P:(n + 1) * P], ident[:, :])
                last.then_inc(block_turned, 1)

            def product(s, u, it):
                b2_ = 2 * (s - BACK_LAG) + u
                if not 0 <= b2_ < 2 * STEPS:
                    return
                j = b2_ + 2 * PERIOD * it
                n = b2_ % BLOCKS
                parity = b2_ // BLOCKS % 2
                pe.wait_ge(lo_done, j + 1)
                if n == 0 and b2_ >= 2 * BLOCKS:
                    pe.wait_ge(right_done, b2_ // BLOCKS - 1 + 2 * it)
                acc = pa[:, parity, :]
                pe.matmul(acc, v_hi[:, n, :], pt_hi[:, b2_ % 2, :], start=n == 0, stop=False)
                pe.matmul(acc, v_lo[:, n, :], pt_hi[:, b2_ % 2, :], start=False, stop=False)
                pe.matmul(acc, v_hi[:, n, :], pt_lo[:, b2_ % 2, :], start=False, stop=n == BLOCKS - 1).then_inc(
                    block_used, 1)

            def step(s, it):
                b = s - FIN_LAG
                if b >= 0 and b % GSTEPS == 0 and b // GSTEPS < GROUPS:
                    g = b // GSTEPS + 2 * it
                    pe.wait_ge(agg_out, g + 1)
                    for i in range(TILES):
                        last = pe.transpose(pa[:, b // GSTEPS % 2, i * P:(i + 1) * P], agg[:, i * P:(i + 1) * P],
                                            ident[:, :])
                    last.then_inc(agg_turned, 1)
                turn(s, 0, it)
                score(s, 0, it)
                product(s, -1, it)
                turn(s, 1, it)
                score(s, 1, it)
                product(s, 0, it)

            main(pe, step)


INPUTS = ["x", "adj", "L0_gnn_neigh", "L0_gnn_Wx1", "L0_gnn_bx1", "L0_gnn_Wx2", "L0_gnn_bx2", "L0_gnn_Wn1",
          "L0_gnn_bn1", "L0_gnn_Wn2", "L0_gnn_bn2", "L0_gnn_Wv", "L0_gnn_bv", "L0_gnn_Wfx", "L0_gnn_bfx"]


def kernel(**inputs):
    import numpy as np
    import concourse.bacc as bacc
    from concourse.bass_utils import run_bass_kernel_spmd

    nc = bacc.Bacc("TRN2", target_bir_lowering=False, num_devices=1, dynamic_dma_scratch_size=1024)
    arrays, args = {}, []
    for name in INPUTS:
        a = np.ascontiguousarray(inputs[name])
        arrays[f"in_{name}"] = a
        args.append(nc.dram_tensor(f"in_{name}", a.shape, mybir.dt.from_np(a.dtype), kind="ExternalInput").ap())
    out = nc.dram_tensor("out_h", (N_X, 2 * D_OUT), FP32, kind="ExternalOutput").ap()
    build(nc, *args, out)
    return run_bass_kernel_spmd(nc, [arrays], core_ids=[0]).results[0]["out_h"]
```

```python
from contextlib import ExitStack

import concourse.bass as bass
from concourse import mybir

FP32 = mybir.dt.float32
FP32R = mybir.dt.float32r
BF16 = mybir.dt.bfloat16
INT32 = mybir.dt.int32
ALU = mybir.AluOpType
ACT = mybir.ActivationFunctionType
AX = mybir.AxisListType

P = 128
N_X, N_NEIGH, D_IN, D_HID, D_OUT = 4096, 4096, 256, 32, 128
KT = D_IN // P
BANK = 512
GROUP = BANK
TILES = GROUP // P
GROUPS = N_X // GROUP
NEIGH_GROUPS = N_NEIGH // GROUP
CHUNK = 2 * BANK
CHUNKS = N_NEIGH // CHUNK
STEPS = GROUPS * TILES * CHUNKS
GSTEPS = TILES * CHUNKS
BLOCKS = N_NEIGH // P
PERIOD = 2 * GSTEPS
EPS = 1e-5
MASKED = -float(2 ** 53)
SLOPE = 0.01
RISE = 99.0

ADJ_RING = 4
DMA_RING = 2048
CONSTS_IN = 16 * 3
B2_IN = 16 * 2 * (P // D_HID)
WIDE_IN = 16 * 2
EXP_LAG = CHUNKS + 1
BACK_LAG = GSTEPS + 3
COPY_LAG = BACK_LAG + GSTEPS
FIN_LAG = COPY_LAG + 1
SUM_LAG = GSTEPS + EXP_LAG + 1
LOOP_START, LOOPS = 2 * GSTEPS + 8, 2
END = STEPS + FIN_LAG - GSTEPS + 2
X_LOAD, X_SUM, X_STATS, X_AGGR, X_RSTD = -8, -6, -7, -4, -3
X_NORM = (-1, 0, 1, 3)
X_TURN = 6
X_FIRST = 8
X_TANH = 11
X_SECOND = 12
X_STACK = 13
X_WIDE, X_LEFT = 15, 18
V_START, V_STRIDE = 2, 2
NEWTON = 3
NEWTON_OPS = 2 + 4 * NEWTON


def build(nc, x, adj, neigh, wx1, bx1, wx2, bx2, wn1, bn1, wn2, bn2, wv, bv, wfx, bfx, out):
    assert LOOP_START + LOOPS * PERIOD <= STEPS - ADJ_RING
    with ExitStack() as ctx:
        def sb(name, shape, dt):
            return ctx.enter_context(nc.sbuf_tensor(name, shape, dt))

        def sem(name):
            return ctx.enter_context(nc.semaphore(name))

        scores = sb("scores", [P, 2 * TILES, N_NEIGH], FP32)
        neib = sb("neib", [P, N_NEIGH], FP32R)
        v_hi = sb("v_hi", [P, BLOCKS, D_OUT], FP32R)
        v_lo = sb("v_lo", [P, BLOCKS, D_OUT], FP32R)
        adj_in = sb("adj_in", [P, ADJ_RING, CHUNK], BF16)
        mask = sb("mask", [P, 2, CHUNK], BF16)
        xs = sb("xs", [P, 2, GROUP], FP32R)
        pt_hi = sb("pt_hi", [P, 2, GROUP], FP32R)
        pt_lo = sb("pt_lo", [P, 2, GROUP], FP32R)
        agg = sb("agg", [P, GROUP], FP32)
        x_right = sb("x_right", [P, TILES, D_OUT], FP32)
        x_left = sb("x_left", [P, 2, TILES * D_OUT], FP32)
        x_rows = sb("x_rows", [P, TILES, D_IN], FP32)
        x_rows_t = sb("x_rows_t", [P, KT, GROUP], FP32)
        w_fx = sb("w_fx", [P, KT, D_OUT], FP32)
        b_fx = sb("b_fx", [P, 1, D_OUT], FP32)
        ident = sb("ident", [P, P], FP32)
        diag = sb("diag", [P, P], BF16)
        top = sb("top", [P, 2, CHUNKS], FP32)
        neg_top = sb("neg_top", [P, 2, 1], FP32)
        sums = sb("sums", [P, 2, TILES, CHUNKS], FP32)
        row_sum = sb("row_sum", [P, TILES], FP32)
        inv_sum = sb("inv_sum", [P, 2, TILES], FP32)
        w1 = sb("w1", [P, 2, KT, D_HID], FP32)
        w2 = sb("w2", [D_HID, 2, P], FP32)
        b1 = sb("b1", [D_HID, 2], FP32)
        b2 = sb("b2", [P, 2], FP32)
        stats = sb("stats", [P, TILES, 6], FP32)
        mean_var = sb("mean_var", [P, TILES, 2], FP32)
        var_eps = sb("var_eps", [P, TILES], FP32)
        factor = sb("factor", [P, TILES], FP32)
        rstd = sb("rstd", [P, TILES], FP32)

        def scratch(buffer, start, *shape):
            n = 1
            for s in shape:
                n *= s
            ap = scores[:, buffer, start:start + n]
            names = " ".join(f"d{i}" for i in range(len(shape)))
            sizes = {f"d{i}": s for i, s in enumerate(shape)}
            return ap.rearrange(f"p ({names}) -> p {names}", **sizes)

        rows = scratch(4, 0, 2, TILES, D_IN)
        hidden = scratch(4, 2048, 2, GROUP)
        w_v = scratch(5, 0, KT, D_OUT)
        b_v = scratch(5, 512, 1, D_OUT)
        value = scratch(5, 1024, 2, TILES * D_OUT)
        rows_t = scores[:, 6:8, :].rearrange("p a (g n) -> p (a g) n", n=KT * GROUP)

        ps = ctx.enter_context(nc.psum_tensor("ps_scores", [P, 2, CHUNK], FP32))
        pt = ctx.enter_context(nc.psum_tensor("ps_turned", [P, 2, BANK], FP32))
        pa = ctx.enter_context(nc.psum_tensor("ps_product", [P, 2, BANK], FP32))
        ps_hidden, ps_att, ps_value = pa[0:D_HID, 0, :], pa[:, 1, :], pa[:, 1, :]

        consts_in, b2_in = [sem("consts_in_neigh"), sem("consts_in_x")], sem("b2_in")
        wide_in = [sem("wide_in_neigh"), sem("wide_in_x")]
        rows_in = [sem("rows_in0"), sem("rows_in1")]
        made = sem("made")
        fills = sem("fills")
        turned = sem("turned")
        turned_out = sem("turned_out")
        first_done = sem("first_done")
        hidden_done = sem("hidden_done")
        wide_done = sem("wide_done")
        wide_out = sem("wide_out")
        second_done = sem("second_done")
        att_hi, att_out = sem("att_hi"), sem("att_out")
        v_hi_done, v_lo_done = sem("v_hi_done"), sem("v_lo_done")
        stats_done, aggr_done = sem("stats_done"), sem("aggr_done")
        joined, pool_joined = sem("joined"), sem("pool_joined")
        newton = sem("newton")
        x_rows_in = sem("x_rows_in")
        x_summed = sem("x_summed")
        x_normed = sem("x_normed")
        x_turned, x_turned_out = sem("x_turned"), sem("x_turned_out")
        x_first, x_hidden = sem("x_first"), sem("x_hidden")
        x_second, x_att_hi, x_att = sem("x_second"), sem("x_att_hi"), sem("x_att")
        x_wide, left_done, left_out = sem("x_wide"), sem("left_done"), sem("left_out")
        adj_ready = [sem(f"adj_ready{i}") for i in range(ADJ_RING)]
        mask_done = sem("mask_done")
        scored = sem("scored")
        risen = sem("risen")
        leaked = sem("leaked")
        top_done = sem("top_done")
        exp_done = sem("exp_done")
        block_turned = sem("block_turned")
        hi_done, lo_done = sem("hi_done"), sem("lo_done")
        block_used = sem("block_used")
        agg_out = sem("agg_out")
        agg_turned = sem("agg_turned")
        row_sum_done, sums_done = sem("row_sum_done"), sem("sums_done")
        right_done = sem("right_done")
        x_right_in = sem("x_right_in")
        right_out = sem("right_out")

        block = ctx.enter_context(nc.Block())

        def encode(engine, step):
            for e in range(2):
                step(e, 0)
            with engine.Fori(1, GROUPS // 2 - 1) as it:
                for e in range(2):
                    step(e, it)
            for e in range(GROUPS - 2, GROUPS):
                step(e, 0)

        def it_is(it, e, group):
            return isinstance(it, int) and e == group

        def wait(engine, semaphore, value):
            if not isinstance(value, int) or value > 0:
                engine.wait_ge(semaphore, value)

        def main(engine, step):
            for s in range(LOOP_START):
                step(s, 0)
            with engine.Fori(0, LOOPS) as it:
                for s in range(LOOP_START, LOOP_START + PERIOD):
                    step(s, it)
            for s in range(LOOP_START + LOOPS * PERIOD, END):
                step(s, 0)

        def x_due(s, stage):
            e = (s - stage) // GSTEPS + 1
            return e if (s - stage) % GSTEPS == 0 and 1 <= e < GROUPS else 0

        def x_bank(e):
            return pa[:, (e + 1) % 2, :] if e else ps[:, 1, 0:BANK]

        def value_due(s):
            v = (s - V_START) // V_STRIDE
            return v if (s - V_START) % V_STRIDE == 0 and 0 <= v < NEIGH_GROUPS else None

        def chunk_of(s):
            return s // GSTEPS % 2, s // CHUNKS % TILES, s % CHUNKS

        def v_halves(v, half):
            return half[:, v * TILES:(v + 1) * TILES, :].rearrange("p t d -> p (t d)")

        @block.sync
        def _(sp):
            x_tiles = x.rearrange("(t p) d -> p t d", p=P)
            neigh_tiles = neigh.rearrange("(t p) d -> p t d", p=P)
            out_tiles = out.rearrange("(t p) d -> p t d", p=P)

            def load_neigh(par, it):
                e = 2 * it + par
                sp.dma_start(rows[:, par], neigh_tiles[:, bass.ds(e * TILES, TILES), :]).then_inc(rows_in[par], 16)

            def load_x_rows(e):
                sp.dma_start(x_rows[:, :, :], x_tiles[:, bass.ds(e * TILES, TILES), :]).then_inc(x_rows_in, 16)

            def load_x_right(g):
                sp.dma_start(x_right[:, :, :],
                             x_tiles[:, bass.ds(g * TILES, TILES), D_OUT:2 * D_OUT]).then_inc(x_right_in, 16)

            load_neigh(0, 0)
            load_x_rows(0)
            load_neigh(1, 0)
            load_x_right(0)
            with sp.Fori(1, NEIGH_GROUPS // 2) as it:
                for par in range(2):
                    sp.wait_ge(turned, KT * (2 * it + par - 1))
                    load_neigh(par, it)

            sp.wait_ge(x_turned, KT)
            sp.wait_ge(x_summed, 1)
            load_x_rows(1)

            def store_left(e0, e):
                sp.wait_ge(left_done, e + 1)
                sp.dma_start(out_tiles[:, bass.ds(e * TILES, TILES), 0:D_OUT],
                             x_left[:, e0 % 2].rearrange("p (t d) -> p t d", d=D_OUT)).then_inc(left_out, 16)

            def step(s, it):
                if e := x_due(s, X_LOAD):
                    sp.wait_ge(x_turned, KT * (e + 2 * it))
                    sp.wait_ge(x_summed, e + 2 * it)
                    load_x_rows(e + 2 * it)
                if s == 3:
                    store_left(0, 0)
                if e := x_due(s, X_LEFT):
                    store_left(e, e + 2 * it)
                if (s - FIN_LAG - 2) % GSTEPS == 0 and s >= FIN_LAG + 2:
                    g0 = (s - FIN_LAG - 2) // GSTEPS
                    g = g0 + 2 * it
                    sp.wait_ge(right_done, g + 1)
                    sp.dma_start(out_tiles[:, bass.ds(g * TILES, TILES), D_OUT:2 * D_OUT],
                                 x_right[:, :, :]).then_inc(right_out, 16)
                    if g0 < GROUPS - 1:
                        sp.wait_ge(right_out, 16 * (g + 1))
                        load_x_right(g + 1)

            main(sp, step)
            sp.wait_ge(right_done, GROUPS)
            sp.dma_start(out_tiles[:, (GROUPS - 1) * TILES:GROUPS * TILES, D_OUT:2 * D_OUT],
                         x_right[:, :, :]).then_inc(right_out, 16)
            sp.wait_ge(left_out, 16 * GROUPS)
            sp.wait_ge(right_out, 16 * GROUPS)

        @block.gpsimd
        def _(pool):
            pool.memset(ident[:, :], 0.0).then_inc(fills, 1)
            pool.memset(diag[:, :], 0.0).then_inc(fills, 1)
            pool.wait_ge(fills, 2)
            pool.affine_select(out=ident[:, :], in_=ident[:, :], compare_op=ALU.not_equal, fill=1.0,
                               base=0, pattern=[[-1, P]], channel_multiplier=1).then_inc(made, 1)
            pool.affine_select(out=diag[:, :], in_=diag[:, :], compare_op=ALU.not_equal, fill=MASKED,
                               base=0, pattern=[[-1, P]], channel_multiplier=1).then_inc(made, 1)

            def left_sum(e0, e):
                pool.wait_ge(x_rows_in, 16 * (e + 1))
                wait(pool, left_out, 16 * (e - 1))
                pool.tensor_tensor(x_left[:, e0 % 2].rearrange("p (t d) -> p t d", d=D_OUT), x_rows[:, :, 0:D_OUT],
                                   b_fx[:, :, :].to_broadcast([P, TILES, D_OUT]), ALU.add).then_inc(x_summed, 1)

            def rstd_of(e):
                ops = [0]

                def ordered(op):
                    op.then_inc(newton, 1)
                    ops[0] += 1
                    if ops[0] < NEWTON_OPS:
                        pool.wait_ge(newton, NEWTON_OPS * e + ops[0])

                pool.wait_ge(aggr_done, e + 1)
                wait(pool, x_normed, TILES * e)
                pool.sem_inc(pool_joined, 1)
                ordered(pool.tensor_scalar(var_eps[:, :], mean_var[:, :, 1], EPS, None, ALU.add))
                pool.sem_inc(pool_joined, 1)
                ordered(pool.tensor_scalar(rstd.bitcast(INT32)[:, :], var_eps.bitcast(INT32)[:, :], -0.5,
                                           float(0x5f3759df), ALU.mult, ALU.add))
                for _ in range(NEWTON):
                    ordered(pool.tensor_tensor(factor[:, :], rstd[:, :], rstd[:, :], ALU.mult))
                    ordered(pool.tensor_tensor(factor[:, :], factor[:, :], var_eps[:, :], ALU.mult))
                    pool.sem_inc(pool_joined, 1)
                    ordered(pool.tensor_scalar(factor[:, :], factor[:, :], -0.5, 1.5, ALU.mult, ALU.add))
                    ordered(pool.tensor_tensor(rstd[:, :], rstd[:, :], factor[:, :], ALU.mult))

            rstd_of(0)
            pool.wait_ge(wide_in[1], WIDE_IN)
            left_sum(0, 0)
            for i in range(ADJ_RING):
                pool.dma_start(adj_in[:, i, :], adj[0:P, i * CHUNK:(i + 1) * CHUNK]).then_inc(adj_ready[i], 16)
            left_sum(1, 1)
            rstd_of(1)

            def step(s, it):
                n = s + ADJ_RING
                if n < STEPS:
                    tile = n // CHUNKS + 2 * TILES * it
                    pool.wait_ge(mask_done, s + 1 + PERIOD * it)
                    pool.dma_start(adj_in[:, n % ADJ_RING, :],
                                   adj[bass.ds(tile * P, P), n % CHUNKS * CHUNK:(n % CHUNKS + 1) * CHUNK]).then_inc(
                        adj_ready[n % ADJ_RING], 16)
                if e := x_due(s, X_SUM):
                    left_sum(e, e + 2 * it)
                if e := x_due(s, X_RSTD):
                    rstd_of(e + 2 * it)
                if value_due(s - 2) is not None:
                    v = value_due(s - 2)
                    pool.wait_ge(v_hi_done, v + 1)
                    pool.tensor_tensor(v_halves(v, v_lo), value[:, v % 2], v_halves(v, v_hi).bitcast(FP32),
                                       ALU.subtract).then_inc(v_lo_done, 1)

            main(pool, step)

        @block.scalar
        def _(act):
            for side, (w, b, v) in enumerate(((wn1, bn1, wn2), (wx1, bx1, wx2))):
                act.dma_start(w1[:, side], w.rearrange("(k p) h -> p k h", p=P)).then_inc(consts_in[side], 16)
                act.dma_start(b1[:, side:side + 1], b.rearrange("(p a) -> p a", a=1)).then_inc(consts_in[side], 16)
                act.dma_start(w2[:, side].rearrange("p (r h) -> p r h", h=D_HID),
                              v.rearrange("p (a h) -> p a h", a=1).to_broadcast([D_HID, P // D_HID, D_HID])).then_inc(
                    consts_in[side], 16)
            for side, c in enumerate((bn2, bx2)):
                for r in range(P // D_HID):
                    act.dma_start(b2[r * D_HID:(r + 1) * D_HID, side:side + 1],
                                  c.rearrange("(p a) -> p a", a=1)).then_inc(b2_in, 16)
            for side, w, b, w_in, b_in in ((1, w_fx, b_fx, wfx, bfx), (0, w_v, b_v, wv, bv)):
                act.dma_start(w[:, :, :], w_in.rearrange("(k p) d -> p k d", p=P)).then_inc(wide_in[side], 16)
                act.dma_start(b[:, :, :], b_in.rearrange("(a b d) -> a b d", a=1, b=1).to_broadcast([P, 1, D_OUT])
                              ).then_inc(wide_in[side], 16)

            def turned_copy(q):
                for k in range(KT):
                    act.wait_ge(turned, KT * q + k + 1)
                    act.activation(rows_t[:, bass.ds(q, 1), k * GROUP:(k + 1) * GROUP].rearrange("p a n -> p (a n)"),
                                   pt[:, k], ACT.Copy).then_inc(turned_out, 1)

            def neigh_step(e, it):
                q = e + 2 * it
                par = e % 2
                act.wait_ge(first_done, q + 1)
                wait(act, second_done, q - 1)
                act.activation(hidden[0:D_HID, par], ps_hidden, ACT.Tanh, bias=b1[:, 0:1]).then_inc(hidden_done, 1)
                if e < NEIGH_GROUPS - 1:
                    turned_copy(q + 1)
                if it_is(it, e, 1):
                    act.wait_ge(consts_in[1], CONSTS_IN)
                    for k in range(KT):
                        x_turned_copy(0, k, x_bank(0))
                if it_is(it, e, NEIGH_GROUPS - 2):
                    x_tanh(0, x_bank(0))

            def x_turned_copy(e, k, bank):
                act.wait_ge(x_turned, KT * e + k + 1)
                if k == 0:
                    wait(act, x_wide, e)
                act.activation(x_rows_t[:, k, :], bank, ACT.Relu).then_inc(x_turned_out, 1)

            def x_tanh(e, bank):
                act.wait_ge(x_first, e + 1)
                wait(act, agg_turned, e - 2)
                act.activation(agg[0:D_HID, :], bank[0:D_HID, :], ACT.Tanh, bias=b1[:, 1:2]).then_inc(x_hidden, 1)

            turned_copy(0)
            act.wait_ge(consts_in[0], CONSTS_IN)
            encode(act, neigh_step)

            def hi(s, u, it):
                b = s - BACK_LAG
                if not 0 <= b < STEPS:
                    return
                j = 2 * b + u + 2 * PERIOD * it
                act.wait_ge(block_turned, j + 1)
                if 2 * b + u >= 2:
                    act.wait_ge(block_used, j - 1)
                act.activation(pt_hi[:, u], pt[:, u], ACT.Copy).then_inc(hi_done, 1)

            def step(s, it):
                k = s + PERIOD * it
                hi(s, 0, it)
                e = s - EXP_LAG
                if 0 <= e < STEPS:
                    parity, tile, c = chunk_of(e)
                    t = e // CHUNKS + 2 * TILES * it
                    if c == 0:
                        act.wait_ge(top_done, t + 1)
                        if tile == 0 and e >= 2 * GSTEPS:
                            act.wait_ge(sums_done, e // GSTEPS - 1 + 2 * it)
                    cols = scores[:, parity * TILES + tile, c * CHUNK:(c + 1) * CHUNK]
                    act.activation(cols, cols, ACT.Exp, bias=neg_top[:, tile % 2, :],
                                   accum_out=sums[:, parity, tile, c:c + 1]).then_inc(exp_done, 1)
                hi(s, 1, it)
                if s < STEPS:
                    parity, tile, c = chunk_of(s)
                    act.wait_ge(scored, k + 1)
                    if s == GSTEPS:
                        act.wait_ge(second_done, NEIGH_GROUPS)
                    if s == GSTEPS + CHUNKS:
                        act.wait_ge(v_lo_done, NEIGH_GROUPS)
                    if tile == 0 and s >= 2 * GSTEPS:
                        act.wait_ge(block_turned, (s // GSTEPS - 2) * BLOCKS + (c + 1) * BLOCKS // CHUNKS + 2 * BLOCKS * it)
                    act.activation(scores[:, parity * TILES + tile, c * CHUNK:(c + 1) * CHUNK], ps[:, s % 2],
                                   ACT.Relu, scale=RISE).then_inc(risen, 1)
                for k in range(KT):
                    if e := x_due(s, X_TURN + k):
                        x_turned_copy(e + 2 * it, k, x_bank(e))
                if e := x_due(s, X_TANH):
                    x_tanh(e + 2 * it, x_bank(e))
                b = s - COPY_LAG
                if b >= 0 and b % GSTEPS == 0 and b // GSTEPS < GROUPS:
                    g = b // GSTEPS + 2 * it
                    act.wait_ge(block_used, (g + 1) * BLOCKS)
                    wait(act, agg_turned, g)
                    act.wait_ge(x_second, min(GROUPS, g + 3) if isinstance(g, int) else g + 3)
                    act.activation(agg[:, :], pa[:, b // GSTEPS % 2], ACT.Copy).then_inc(agg_out, 1)

            main(act, step)

        @block.vector
        def _(dve):
            def x_stats(e, i):
                dve.wait_ge(x_rows_in, 16 * (e + 1))
                wait(dve, aggr_done, e)
                dve.bn_stats(stats[:, i, :], x_rows[:, i, :]).then_inc(stats_done, 1)

            def x_aggr(e):
                dve.wait_ge(stats_done, TILES * (e + 1))
                wait(dve, x_normed, TILES * e)
                wait(dve, newton, NEWTON_OPS * e)
                dve.sem_inc(joined, 1)
                for i in range(TILES):
                    last = dve.bn_aggr(mean_var[:, i, :], stats[:, i, :])
                last.then_inc(aggr_done, 1)

            def neigh_step(e, it):
                q = e + 2 * it
                if it_is(it, e, NEIGH_GROUPS - 2):
                    for i in range(TILES):
                        x_stats(1, i)
                    x_aggr(1)
                if it_is(it, e, NEIGH_GROUPS - 1):
                    mask_of(0, 0)
                    mask_of(1, 0)
                    x_normalise(1, 0)
                    x_stack_high(0, 0, x_bank(0))
                    x_stack_low(0, 0, x_bank(0))
                dve.wait_ge(second_done, q + 1)
                cols = neib[:, bass.ds(q * GROUP, GROUP)]
                dve.tensor_scalar(cols, ps_att, b2[:, 0:1], None, ALU.add).then_inc(att_hi, 1)
                dve.wait_ge(att_hi, q + 1)
                for p in (D_HID, 3 * D_HID):
                    part = neib[p:p + D_HID, bass.ds(q * GROUP, GROUP)]
                    last = dve.scalar_tensor_tensor(part, pa[p:p + D_HID, 1, :], b2[p:p + D_HID, 0:1],
                                                    part.bitcast(FP32), ALU.add, ALU.subtract)
                last.then_inc(att_out, 1)

            def x_normalise(e, i):
                dve.wait_ge(newton, NEWTON_OPS * (e + 1))
                dve.wait_ge(x_summed, e + 1)
                dve.tensor_scalar(x_rows[:, i, :], x_rows[:, i, :], mean_var[:, i, 0:1],
                                  rstd[:, i:i + 1], ALU.subtract, ALU.mult).then_inc(x_normed, 1)

            def x_stack_high(e, par, bank):
                dve.wait_ge(x_second, e + 1)
                wait(dve, scored, GSTEPS * (e - 1))
                dve.tensor_scalar(xs[:, par, :], bank, b2[:, 1:2], None, ALU.add).then_inc(x_att_hi, 1)

            def x_stack_low(e, par, bank):
                dve.wait_ge(x_att_hi, e + 1)
                low = xs[P // 2:P, par, :]
                dve.scalar_tensor_tensor(low, bank[P // 2:P, :], b2[P // 2:P, 1:2], low.bitcast(FP32),
                                         ALU.add, ALU.subtract).then_inc(x_att, 1)

            def x_left_out(e, e0, bank):
                dve.wait_ge(x_wide, e + 1)
                dve.tensor_tensor(x_left[:, e0 % 2], bank, x_left[:, e0 % 2], ALU.add).then_inc(left_done, 1)

            def value_out(v):
                dve.wait_ge(wide_done, v + 1)
                if v >= 2:
                    dve.wait_ge(v_lo_done, v - 1)
                dve.tensor_tensor(value[:, v % 2].rearrange("p (t d) -> p t d", d=D_OUT),
                                  ps_value.rearrange("p (t d) -> p t d", d=D_OUT),
                                  b_v[:, :, :].to_broadcast([P, TILES, D_OUT]), ALU.add).then_inc(wide_out, 1)
                dve.wait_ge(wide_out, v + 1)
                dve.tensor_copy(v_halves(v, v_hi), value[:, v % 2]).then_inc(v_hi_done, 1)

            for i in range(TILES):
                x_stats(0, i)
            x_aggr(0)
            for i in range(TILES):
                x_normalise(0, i)
            dve.wait_ge(b2_in, B2_IN)

            def mask_of(n, it):
                k = n + PERIOD * it
                dve.wait_ge(adj_ready[n % ADJ_RING], 16 * (n // ADJ_RING + 1) + 16 * PERIOD // ADJ_RING * it)
                if n >= 2:
                    dve.wait_ge(scored, k - 1)
                dve.tensor_scalar(mask[:, n % 2, :], adj_in[:, n % ADJ_RING, :], 0.0, None, ALU.is_le).then_inc(
                    mask_done, 1)

            def lo(s, u, it):
                b = s - BACK_LAG
                if not 0 <= b < STEPS:
                    return
                j = 2 * b + u + 2 * PERIOD * it
                dve.wait_ge(hi_done, j + 1)
                dve.tensor_tensor(pt_lo[:, u], pt[:, u], pt_hi[:, u].bitcast(FP32), ALU.subtract).then_inc(
                    lo_done, 1)

            def step(s, it):
                lo(s, 0, it)
                n = s - 1
                if 0 <= n < STEPS:
                    parity, tile, c = chunk_of(n)
                    k = n + PERIOD * it
                    cols = scores[:, parity * TILES + tile, c * CHUNK:(c + 1) * CHUNK]
                    dve.wait_ge(risen, k + 1)
                    if c:
                        dve.wait_ge(leaked, k)
                    start = top[:, tile % 2, c - 1:c] if c else -3.0e38
                    if c == 0 and n >= 2 * CHUNKS:
                        dve.wait_ge(top_done, n // CHUNKS - 1 + 2 * TILES * it)
                    dve.sem_inc(joined, 1)
                    dve.tensor_tensor_reduce(cols, ps[:, n % 2], cols, SLOPE, start, ALU.add, ALU.max,
                                             top[:, tile % 2, c:c + 1]).then_inc(leaked, 1)
                if 0 <= n < STEPS and n % CHUNKS == CHUNKS - 1:
                    dve.wait_ge(leaked, n + 1 + PERIOD * it)
                    if n >= 2 * CHUNKS:
                        dve.wait_ge(exp_done, (n // CHUNKS - 1) * CHUNKS + PERIOD * it)
                    dve.tensor_scalar(neg_top[:, n // CHUNKS % 2, :], top[:, n // CHUNKS % 2, CHUNKS - 1:CHUNKS],
                                      -1.0, None, ALU.mult).then_inc(top_done, 1)
                lo(s, 1, it)
                if s + 2 < STEPS:
                    mask_of(s + 2, it)
                for i in range(TILES):
                    if e := x_due(s, X_STATS + i):
                        x_stats(e + 2 * it, i)
                    if e := x_due(s, X_NORM[i]):
                        x_normalise(e + 2 * it, i)
                if e := x_due(s, X_AGGR):
                    x_aggr(e + 2 * it)
                if e := x_due(s, X_STACK):
                    x_stack_high(e + 2 * it, e % 2, x_bank(e))
                if e := x_due(s, X_STACK + 1):
                    x_stack_low(e + 2 * it, e % 2, x_bank(e))
                if s == 1:
                    x_left_out(0, 0, pa[:, 1, :])
                if e := x_due(s, X_LEFT):
                    x_left_out(e + 2 * it, e, x_bank(e))
                if value_due(s - 1) is not None:
                    value_out(value_due(s - 1))
                b = s - SUM_LAG
                if b >= 0 and b % GSTEPS == 0 and b // GSTEPS < GROUPS:
                    g = b // GSTEPS + 2 * it
                    parity = b // GSTEPS % 2
                    dve.wait_ge(exp_done, (g + 1) * GSTEPS)
                    if b:
                        dve.wait_ge(sums_done, g)
                    dve.reduce_sum(row_sum[:, :], sums[:, parity], axis=AX.X).then_inc(row_sum_done, 1)
                    dve.wait_ge(row_sum_done, g + 1)
                    if b:
                        dve.wait_ge(right_done, g)
                    dve.reciprocal(inv_sum[:, parity, :], row_sum[:, :]).then_inc(sums_done, 1)
                b = s - FIN_LAG
                if b >= 0 and b % GSTEPS < 2 and b // GSTEPS < GROUPS:
                    g = b // GSTEPS + 2 * it
                    parity = b // GSTEPS % 2
                    if b % GSTEPS == 0:
                        dve.wait_ge(agg_turned, g + 1)
                        dve.wait_ge(sums_done, g + 1)
                        dve.wait_ge(x_right_in, 16 * (g + 1))
                    for i in range(b % GSTEPS * TILES // 2, (b % GSTEPS + 1) * TILES // 2):
                        last = dve.scalar_tensor_tensor(
                            x_right[:, i, :], pa[:, parity, i * P:(i + 1) * P], inv_sum[:, parity, i:i + 1],
                            x_right[:, i, :], ALU.mult, ALU.add)
                    if b % GSTEPS == 1:
                        last.then_inc(right_done, 1)

            encode(dve, neigh_step)
            dve.wait_ge(wide_in[0], WIDE_IN)
            main(dve, step)

        @block.tensor
        def _(pe):
            def turn_rows(q, e, it):
                par = e % 2
                pe.wait_ge(rows_in[par], 16 * (e // 2 + it + 1))
                for k in range(KT):
                    wait(pe, turned_out, KT * (q - 1) + k + 1)
                    for i in range(TILES):
                        last = pe.transpose(pt[:, k, i * P:(i + 1) * P], rows[:, par, i, k * P:(k + 1) * P],
                                            ident[:, :])
                    last.then_inc(turned, 1)

            def neigh_step(e, it):
                q = e + 2 * it
                par = e % 2
                pe.wait_ge(turned_out, KT * (q + 1))
                wait(pe, hidden_done, q)
                for k in range(KT):
                    last = pe.matmul(ps_hidden, w1[:, 0, k, :],
                                     rows_t[:, bass.ds(q, 1), k * GROUP:(k + 1) * GROUP].rearrange("p a n -> p (a n)"),
                                     start=k == 0, stop=k == KT - 1)
                last.then_inc(first_done, 1)
                if e < NEIGH_GROUPS - 1:
                    turn_rows(q + 1, e + 1, it)
                if it_is(it, e, 1):
                    pe.wait_ge(consts_in[1], CONSTS_IN)
                    for k in range(KT):
                        x_turn(0, k, x_bank(0))
                if it_is(it, e, NEIGH_GROUPS - 2):
                    for i in range(2 * KT):
                        x_first_layer(0, i, x_bank(0))
                if it_is(it, e, NEIGH_GROUPS - 1):
                    for h in range(2):
                        x_second_layer(0, h, x_bank(0))
                pe.wait_ge(hidden_done, q + 1)
                wait(pe, att_out, q)
                pe.matmul(ps_att, w2[:, 0, :], hidden[0:D_HID, par], start=True, stop=True).then_inc(
                    second_done, 1)

            def value_layer(v):
                if v == 0:
                    pe.wait_ge(wide_in[0], WIDE_IN)
                    pe.wait_ge(left_done, 1)
                else:
                    pe.wait_ge(wide_out, v)
                for i in range(TILES):
                    for k in range(KT):
                        last = pe.matmul(ps_value[:, i * D_OUT:(i + 1) * D_OUT],
                                         rows_t[:, v, k * GROUP + i * P:k * GROUP + (i + 1) * P],
                                         w_v[:, k, :], start=k == 0, stop=k == KT - 1)
                last.then_inc(wide_done, 1)

            def x_turn(e, k, bank):
                if k == 0:
                    pe.wait_ge(x_normed, TILES * (e + 1))
                    wait(pe, right_done, e - 2)
                else:
                    pe.wait_ge(x_turned_out, KT * e + k)
                for i in range(TILES):
                    last = pe.transpose(bank[:, i * P:(i + 1) * P], x_rows[:, i, k * P:(k + 1) * P], ident[:, :])
                last.then_inc(x_turned, 1)

            def x_first_layer(e, i, bank):
                h, k = i // KT, i % KT
                half = slice(h * BANK // 2, (h + 1) * BANK // 2)
                pe.wait_ge(x_turned_out, KT * (e + 1))
                last = pe.matmul(bank[0:D_HID, half], w1[:, 1, k, :], x_rows_t[:, k, half],
                                 start=k == 0, stop=k == KT - 1)
                if i == 2 * KT - 1:
                    last.then_inc(x_first, 1)

            def x_second_layer(e, h, bank):
                half = slice(h * BANK // 2, (h + 1) * BANK // 2)
                pe.wait_ge(x_hidden, e + 1)
                last = pe.matmul(bank[:, half], w2[:, 1, :], agg[0:D_HID, half], start=True, stop=True)
                if h:
                    last.then_inc(x_second, 1)

            def x_wide_layer(e, tiles, bank):
                pe.wait_ge(x_att, e + 1)
                for i in tiles:
                    for k in range(KT):
                        last = pe.matmul(bank[:, i * D_OUT:(i + 1) * D_OUT], x_rows_t[:, k, i * P:(i + 1) * P],
                                         w_fx[:, k, :], start=k == 0, stop=k == KT - 1)
                if i == TILES - 1:
                    last.then_inc(x_wide, 1)

            pe.wait_ge(made, 2)
            turn_rows(0, 0, 0)
            pe.wait_ge(consts_in[0], CONSTS_IN)
            encode(pe, neigh_step)

            def score(s, h, it):
                if s >= STEPS:
                    return
                k = s + PERIOD * it
                parity, tile, c = chunk_of(s)
                if h == 0:
                    pe.wait_ge(mask_done, k + 1)
                    if s >= 2:
                        pe.wait_ge(leaked, k - 1)
                    if s < CHUNKS:
                        pe.wait_ge(att_out, (s + 1) * CHUNK // GROUP)
                    if tile == 0 and c == 0:
                        pe.wait_ge(x_att, s // GSTEPS + 2 * it + 1)
                half = slice(h * BANK, (h + 1) * BANK)
                pe.matmul(ps[:, s % 2, half], diag[:, :], mask[:, s % 2, half], start=True, stop=False)
                last = pe.matmul(ps[:, s % 2, half], xs[:, parity, tile * P:(tile + 1) * P],
                                 neib[:, c * CHUNK + h * BANK:c * CHUNK + (h + 1) * BANK], start=False, stop=True)
                if h == 1:
                    last.then_inc(scored, 1)

            def turn(s, u, it):
                b = s - BACK_LAG
                if not 0 <= b < STEPS:
                    return
                parity = b // GSTEPS % 2
                n = 2 * (b % GSTEPS) + u
                j = 2 * b + u + 2 * PERIOD * it
                per_chunk = BLOCKS // CHUNKS
                if n % per_chunk == 0:
                    pe.wait_ge(exp_done, (b // GSTEPS + 1) * GSTEPS - CHUNKS + n // per_chunk + 1 + PERIOD * it)
                if 2 * b + u >= 2:
                    pe.wait_ge(lo_done, j - 1)
                for i in range(TILES):
                    last = pe.transpose(pt[:, u, i * P:(i + 1) * P],
                                        scores[:, parity * TILES + i, n * P:(n + 1) * P], ident[:, :])
                last.then_inc(block_turned, 1)

            def product(s, u, it):
                b2_ = 2 * (s - BACK_LAG) + u
                if not 0 <= b2_ < 2 * STEPS:
                    return
                j = b2_ + 2 * PERIOD * it
                n = b2_ % BLOCKS
                parity = b2_ // BLOCKS % 2
                pe.wait_ge(lo_done, j + 1)
                if b2_ == 0:
                    pe.wait_ge(v_lo_done, NEIGH_GROUPS)
                if n == 0:
                    g = b2_ // BLOCKS + 2 * it
                    wait(pe, right_done, g - 1)
                    pe.wait_ge(left_done, min(GROUPS, g + 2) if isinstance(g, int) else g + 2)
                acc = pa[:, parity, :]
                pe.matmul(acc, v_hi[:, n, :], pt_hi[:, b2_ % 2, :], start=n == 0, stop=False)
                pe.matmul(acc, v_lo[:, n, :], pt_hi[:, b2_ % 2, :], start=False, stop=False)
                pe.matmul(acc, v_hi[:, n, :], pt_lo[:, b2_ % 2, :], start=False, stop=n == BLOCKS - 1).then_inc(
                    block_used, 1)

            def step(s, it):
                turn(s, 0, it)
                product(s, -2, it)
                score(s, 0, it)
                score(s, 1, it)
                turn(s, 1, it)
                product(s, -1, it)
                b = s - FIN_LAG
                if b >= 0 and b % GSTEPS == 0 and b // GSTEPS < GROUPS:
                    g = b // GSTEPS + 2 * it
                    pe.wait_ge(agg_out, g + 1)
                    for i in range(TILES):
                        last = pe.transpose(pa[:, b // GSTEPS % 2, i * P:(i + 1) * P], agg[:, i * P:(i + 1) * P],
                                            ident[:, :])
                    last.then_inc(agg_turned, 1)
                if s == 0:
                    pe.wait_ge(att_out, NEIGH_GROUPS)
                    pe.wait_ge(wide_in[1], WIDE_IN)
                    x_wide_layer(0, range(TILES), pa[:, 1, :])
                for i in range(2):
                    if e := x_due(s, X_TURN + i):
                        x_turn(e + 2 * it, i, x_bank(e))
                    if e := x_due(s, X_SECOND + i):
                        x_second_layer(e + 2 * it, i, x_bank(e))
                for i in range(2 * KT):
                    if e := x_due(s, X_FIRST + i):
                        x_first_layer(e + 2 * it, i, x_bank(e))
                for i in range(TILES):
                    if e := x_due(s, X_WIDE + i):
                        x_wide_layer(e + 2 * it, [i], x_bank(e))
                if value_due(s) is not None:
                    value_layer(value_due(s))

            main(pe, step)


INPUTS = ["x", "adj", "L0_gnn_neigh", "L0_gnn_Wx1", "L0_gnn_bx1", "L0_gnn_Wx2", "L0_gnn_bx2", "L0_gnn_Wn1",
          "L0_gnn_bn1", "L0_gnn_Wn2", "L0_gnn_bn2", "L0_gnn_Wv", "L0_gnn_bv", "L0_gnn_Wfx", "L0_gnn_bfx"]


def kernel(**inputs):
    import numpy as np
    import concourse.bacc as bacc
    from concourse.bass_utils import run_bass_kernel_spmd

    nc = bacc.Bacc("TRN2", target_bir_lowering=False, num_devices=1, dynamic_dma_scratch_size=DMA_RING)
    arrays, args = {}, []
    for name in INPUTS:
        a = np.ascontiguousarray(inputs[name])
        arrays[f"in_{name}"] = a
        args.append(nc.dram_tensor(f"in_{name}", a.shape, mybir.dt.from_np(a.dtype), kind="ExternalInput").ap())
    out = nc.dram_tensor("out_h", (N_X, 2 * D_OUT), FP32, kind="ExternalOutput").ap()
    build(nc, *args, out)
    return run_bass_kernel_spmd(nc, [arrays], core_ids=[0]).results[0]["out_h"]
```

```python
from contextlib import ExitStack

import concourse.bass as bass
from concourse import mybir

FP32 = mybir.dt.float32
FP32R = mybir.dt.float32r
BF16 = mybir.dt.bfloat16
INT32 = mybir.dt.int32
ALU = mybir.AluOpType
ACT = mybir.ActivationFunctionType
AX = mybir.AxisListType

P = 128
N_X, N_NEIGH, D_IN, D_HID, D_OUT = 4096, 4096, 256, 32, 128
KT = D_IN // P
BANK = 512
GROUP = BANK
TILES = GROUP // P
GROUPS = N_X // GROUP
NEIGH_GROUPS = N_NEIGH // GROUP
CHUNK = 2 * BANK
CHUNKS = N_NEIGH // CHUNK
STEPS = GROUPS * TILES * CHUNKS
GSTEPS = TILES * CHUNKS
BLOCKS = N_NEIGH // P
PERIOD = 2 * GSTEPS
EPS = 1e-5
MASKED = -float(2 ** 53)
SLOPE = 0.01
RISE = 99.0

LOAD = 2
ADJ_RING = 4
HI_RING = 4
DMA_RING = 1024
CONSTS_IN = 16 * 4, 16 * 3
B2_IN = 16 * 2
WIDE_IN = 16 * 2
EXP_LAG = CHUNKS + 1
BACK_LAG = GSTEPS + 3
COPY_LAG = BACK_LAG + GSTEPS + 1
FIN_LAG = COPY_LAG
SUM_LAG = GSTEPS + EXP_LAG + 1
LOOP_START, LOOPS = 2 * GSTEPS + 7, 2
END = STEPS + FIN_LAG - GSTEPS + 2
X_LOAD, X_STATS, X_AGGR = -8, -7, -3
X_RSTD = (-3, -3, -2, -1)
X_NORM = (1, 1, 3, 3)
X_TURN = 6
X_FIRST = 8
X_TANH = 11
X_SECOND = 12
X_STACK = 13
X_WIDE, X_LEFT = 15, 18
X_LEFT_LOAD, X_SUM = 4, 9
V_START, V_STRIDE = 1, 2
POOL_MASKS = BACK_LAG
WARM_UP = 12
NEWTON = 3
NEWTON_OPS = 2 + 4 * NEWTON


def build(nc, x, adj, neigh, wx1, bx1, wx2, bx2, wn1, bn1, wn2, bn2, wv, bv, wfx, bfx, out):
    assert LOOP_START + LOOPS * PERIOD <= STEPS - ADJ_RING
    with ExitStack() as ctx:
        def sb(name, shape, dt):
            return ctx.enter_context(nc.sbuf_tensor(name, shape, dt))

        def sem(name):
            return ctx.enter_context(nc.semaphore(name))

        scores = sb("scores", [P, 2 * TILES, N_NEIGH], FP32)
        neib = sb("neib", [P, N_NEIGH], FP32R)
        v_hi = sb("v_hi", [P, BLOCKS, D_OUT], FP32R)
        v_lo = sb("v_lo", [P, BLOCKS, D_OUT], FP32R)
        adj_in = sb("adj_in", [P, ADJ_RING, CHUNK], BF16)
        mask = sb("mask", [P, 2, CHUNK], BF16)
        xs = sb("xs", [P, 2, GROUP], FP32R)
        pt_hi = sb("pt_hi", [P, HI_RING, GROUP], FP32R)
        pt_lo = sb("pt_lo", [P, 2, GROUP], FP32R)
        agg = sb("agg", [P, GROUP], FP32)
        x_right = sb("x_right", [P, TILES, D_OUT], FP32)
        x_left = sb("x_left", [P, TILES * D_OUT], FP32)
        x_rows = sb("x_rows", [P, TILES, D_IN], FP32)
        x_rows_t = sb("x_rows_t", [P, KT, GROUP], FP32)
        w_fx = sb("w_fx", [P, KT, D_OUT], FP32)
        b_fx = sb("b_fx", [P, 1, D_OUT], FP32)
        ident = sb("ident", [P, P], FP32)
        ident_bf16 = sb("ident_bf16", [P, P], BF16)
        top = sb("top", [P, 2, CHUNKS], FP32)
        neg_top = sb("neg_top", [P, 2, 1], FP32)
        sums = sb("sums", [P, 2, TILES, CHUNKS], FP32)
        row_sum = sb("row_sum", [P, TILES], FP32)
        inv_sum = sb("inv_sum", [P, 2, TILES], FP32)
        w1_x = sb("w1_x", [P, KT, D_HID], FP32)
        w2_x = sb("w2_x", [D_HID, P], FP32)
        b1 = sb("b1", [P, 2], FP32)
        b2 = sb("b2", [P, 2], FP32)
        ones = sb("ones", [1, P], FP32)
        stats = sb("stats", [P, TILES, 6], FP32)
        mean_var = sb("mean_var", [P, TILES, 2], FP32)
        var_eps = sb("var_eps", [P, TILES], FP32)
        factor = sb("factor", [P, TILES], FP32)
        rstd = sb("rstd", [P, TILES], FP32)

        def scratch(buffer, start, *shape):
            n = 1
            for s in shape:
                n *= s
            ap = scores[:, buffer, start:start + n]
            names = " ".join(f"d{i}" for i in range(len(shape)))
            sizes = {f"d{i}": s for i, s in enumerate(shape)}
            return ap.rearrange(f"p ({names}) -> p {names}", **sizes)

        rows = scratch(4, 0, 2, TILES, D_IN)
        hidden = scratch(4, 2048, 2, GROUP)
        w1_n = scratch(4, 3072, KT, P)
        w2_n = scratch(4, 3328, D_HID)
        x_ahead = scratch(5, 3072, TILES, D_IN)
        w_v = scratch(5, 0, KT, D_OUT)
        b_v = scratch(5, 512, 1, D_OUT)
        hidden_stack = pt_hi[:, 0:2, :]
        w2_stack = pt_lo[:, 0, 0:P]
        rows_t = scores[:, 6:8, :].rearrange("p a (g n) -> p (a g) n", n=KT * GROUP)

        ps = ctx.enter_context(nc.psum_tensor("ps_scores", [P, 2, CHUNK], FP32))
        pt = ctx.enter_context(nc.psum_tensor("ps_turned", [P, 2, BANK], FP32))
        pa = ctx.enter_context(nc.psum_tensor("ps_product", [P, 2, BANK], FP32))
        ps_hidden, ps_value = pa[:, 0, :], pt
        ps_att = [ps[:, 1, BANK:CHUNK], pa[:, 1, :]]

        consts_in, b2_in = [sem("consts_in_neigh"), sem("consts_in_x")], sem("b2_in")
        wide_in = [sem("wide_in_neigh"), sem("wide_in_x")]
        rows_in = [sem("rows_in0"), sem("rows_in1")]
        made = sem("made")
        fills = sem("fills")
        turned = sem("turned")
        turned_out = sem("turned_out")
        first_done = sem("first_done")
        hidden_done = sem("hidden_done")
        hidden_hi, hidden_lo = sem("hidden_hi"), sem("hidden_lo")
        w2_hi, w2_done = sem("w2_hi"), sem("w2_done")
        wide_done = sem("wide_done")
        second_done = sem("second_done")
        att_hi, att_out = sem("att_hi"), sem("att_out")
        v_hi_done, v_lo_done = sem("v_hi_done"), sem("v_lo_done")
        stats_done, aggr_done = sem("stats_done"), sem("aggr_done")
        joined, pool_joined = sem("joined"), sem("pool_joined")
        newton = sem("newton")
        x_rows_in, x_ahead_in = sem("x_rows_in"), sem("x_ahead_in")
        x_left_in = sem("x_left_in")
        x_summed = sem("x_summed")
        x_normed = sem("x_normed")
        x_turned, x_turned_out = sem("x_turned"), sem("x_turned_out")
        x_first, x_hidden = sem("x_first"), sem("x_hidden")
        x_second, x_att_hi, x_att = sem("x_second"), sem("x_att_hi"), sem("x_att")
        x_wide, left_done, left_out = sem("x_wide"), sem("left_done"), sem("left_out")
        adj_ready = [sem(f"adj_ready{i}") for i in range(ADJ_RING // LOAD)]
        mask_done = sem("mask_done")
        scored = sem("scored")
        risen = sem("risen")
        masked = sem("masked")
        leaked = sem("leaked")
        top_done = sem("top_done")
        exp_done = sem("exp_done")
        block_turned = sem("block_turned")
        hi_done, lo_done = sem("hi_done"), sem("lo_done")
        block_used = sem("block_used")
        agg_out = sem("agg_out")
        agg_turned = sem("agg_turned")
        row_sum_done, sums_done = sem("row_sum_done"), sem("sums_done")
        right_done = sem("right_done")
        x_right_in = sem("x_right_in")
        right_out = sem("right_out")

        block = ctx.enter_context(nc.Block())

        def encode(engine, step):
            for e in range(2):
                step(e, 0)
            with engine.Fori(1, GROUPS // 2 - 1) as it:
                for e in range(2):
                    step(e, it)
            for e in range(GROUPS - 2, GROUPS):
                step(e, 0)

        def it_is(it, e, group):
            return isinstance(it, int) and e == group

        def wait(engine, semaphore, value):
            if not isinstance(value, int) or value > 0:
                engine.wait_ge(semaphore, value)

        def main(engine, step):
            for s in range(LOOP_START):
                step(s, 0)
            with engine.Fori(0, LOOPS) as it:
                for s in range(LOOP_START, LOOP_START + PERIOD):
                    step(s, it)
            for s in range(LOOP_START + LOOPS * PERIOD, END):
                step(s, 0)

        def x_due(s, stage):
            e = (s - stage) // GSTEPS + 1
            return e if (s - stage) % GSTEPS == 0 and 1 <= e < GROUPS else 0

        def x_bank(e):
            return pa[:, (e + 1) % 2, :] if e else ps[:, 1, 0:BANK]

        def value_due(s):
            v = (s - V_START) // V_STRIDE
            return v if (s - V_START) % V_STRIDE == 0 and 0 <= v < NEIGH_GROUPS else None

        def chunk_of(s):
            return s // GSTEPS % 2, s // CHUNKS % TILES, s % CHUNKS

        def v_halves(v, half):
            return half[:, v * TILES:(v + 1) * TILES, :].rearrange("p t d -> p (t d)")

        @block.sync
        def _(sp):
            x_tiles = x.rearrange("(t p) d -> p t d", p=P)
            neigh_tiles = neigh.rearrange("(t p) d -> p t d", p=P)
            out_tiles = out.rearrange("(t p) d -> p t d", p=P)

            def load_neigh(par, it):
                e = 2 * it + par
                sp.dma_start(rows[:, par], neigh_tiles[:, bass.ds(e * TILES, TILES), :]).then_inc(rows_in[par], 16)

            def load_x_rows(e):
                sp.dma_start(x_rows[:, :, :], x_tiles[:, bass.ds(e * TILES, TILES), :]).then_inc(x_rows_in, 16)

            def load_x_left(g):
                sp.dma_start(x_left.rearrange("p (t d) -> p t d", d=D_OUT),
                             x_tiles[:, bass.ds(g * TILES, TILES), 0:D_OUT]).then_inc(x_left_in, 16)

            def load_x_right(g):
                sp.dma_start(x_right[:, :, :],
                             x_tiles[:, bass.ds(g * TILES, TILES), D_OUT:2 * D_OUT]).then_inc(x_right_in, 16)

            load_neigh(0, 0)
            for k in range(KT):
                sp.dma_start(w1_n[:, k].rearrange("p (r h) -> p r h", h=D_HID),
                             wn1[k * P:(k + 1) * P, :].rearrange("p (r h) -> p r h", r=1).to_broadcast(
                                 [P, P // D_HID, D_HID])).then_inc(consts_in[0], 16)
            sp.dma_start(b1[:, 0:1], bn1.rearrange("(r p a) -> r p a", r=1, a=1).to_broadcast(
                [P // D_HID, D_HID, 1])).then_inc(consts_in[0], 16)
            load_neigh(1, 0)
            load_x_rows(0)
            sp.dma_start(w2_n, wn2.rearrange("(r p) h -> r p h", r=1).to_broadcast(
                [P // D_HID, D_HID, D_HID])).then_inc(consts_in[0], 16)
            sp.dma_start(w1_x[:, :, :], wx1.rearrange("(k p) h -> p k h", p=P)).then_inc(consts_in[1], 16)
            sp.dma_start(b1[0:D_HID, 1:2], bx1.rearrange("(p a) -> p a", a=1)).then_inc(consts_in[1], 16)
            sp.dma_start(w2_x.rearrange("p (r h) -> p r h", h=D_HID),
                         wx2.rearrange("p (a h) -> p a h", a=1).to_broadcast([D_HID, P // D_HID, D_HID])).then_inc(
                consts_in[1], 16)
            sp.dma_start(x_ahead, x_tiles[:, TILES:2 * TILES, :]).then_inc(x_ahead_in, 16)
            for side, c in enumerate((bn2, bx2)):
                sp.dma_start(b2[:, side:side + 1],
                             c.rearrange("(r p a) -> r p a", r=1, a=1).to_broadcast([P // D_HID, D_HID, 1])).then_inc(
                    b2_in, 16)
            with sp.Fori(1, NEIGH_GROUPS // 2) as it:
                for par in range(2):
                    sp.wait_ge(turned, KT * (2 * it + par - 1))
                    load_neigh(par, it)
            for side, w, b, w_in, b_in in ((1, w_fx, b_fx, wfx, bfx), (0, w_v, b_v, wv, bv)):
                sp.dma_start(w[:, :, :], w_in.rearrange("(k p) d -> p k d", p=P)).then_inc(wide_in[side], 16)
                sp.dma_start(b[:, :, :], b_in.rearrange("(a b d) -> a b d", a=1, b=1).to_broadcast([P, 1, D_OUT])
                             ).then_inc(wide_in[side], 16)
            load_x_left(0)
            load_x_right(0)

            sp.wait_ge(x_turned, KT)
            load_x_rows(1)

            def store_left(e):
                sp.wait_ge(left_done, e + 1)
                sp.dma_start(out_tiles[:, bass.ds(e * TILES, TILES), 0:D_OUT],
                             x_left.rearrange("p (t d) -> p t d", d=D_OUT)).then_inc(left_out, 16)

            def step(s, it):
                if e := x_due(s, X_LOAD):
                    sp.wait_ge(x_turned, KT * (e + 2 * it))
                    load_x_rows(e + 2 * it)
                if s == 3:
                    store_left(0)
                if e := x_due(s, X_LEFT):
                    store_left(e + 2 * it)
                if e := x_due(s, X_LEFT_LOAD):
                    sp.wait_ge(left_out, 16 * (e + 2 * it))
                    load_x_left(e + 2 * it)
                if (s - FIN_LAG - 2) % GSTEPS == 0 and s >= FIN_LAG + 2:
                    g0 = (s - FIN_LAG - 2) // GSTEPS
                    g = g0 + 2 * it
                    sp.wait_ge(right_done, g + 1)
                    sp.dma_start(out_tiles[:, bass.ds(g * TILES, TILES), D_OUT:2 * D_OUT],
                                 x_right[:, :, :]).then_inc(right_out, 16)
                    if g0 < GROUPS - 1:
                        sp.wait_ge(right_out, 16 * (g + 1))
                        load_x_right(g + 1)

            main(sp, step)
            sp.wait_ge(right_done, GROUPS)
            sp.dma_start(out_tiles[:, (GROUPS - 1) * TILES:GROUPS * TILES, D_OUT:2 * D_OUT],
                         x_right[:, :, :]).then_inc(right_out, 16)
            sp.wait_ge(left_out, 16 * GROUPS)
            sp.wait_ge(right_out, 16 * GROUPS)

        @block.gpsimd
        def _(pool):
            pool.memset(ident[:, :], 0.0).then_inc(fills, 1)
            pool.memset(ident_bf16[:, :], 0.0).then_inc(fills, 1)
            pool.memset(ones[:, :], 1.0).then_inc(made, 1)
            pool.wait_ge(fills, 2)
            pool.affine_select(out=ident[:, :], in_=ident[:, :], compare_op=ALU.not_equal, fill=1.0,
                               base=0, pattern=[[-1, P]], channel_multiplier=1).then_inc(made, 1)
            pool.affine_select(out=ident_bf16[:, :], in_=ident_bf16[:, :], compare_op=ALU.not_equal, fill=1.0,
                               base=0, pattern=[[-1, P]], channel_multiplier=1).then_inc(made, 1)

            def left_sum(e, h):
                pool.wait_ge(x_left_in, 16 * (e + 1))
                half = x_left.rearrange("p (t d) -> p t d", d=D_OUT)[:, h * TILES // 2:(h + 1) * TILES // 2]
                pool.tensor_tensor(half, half, b_fx[:, :, :].to_broadcast([P, TILES // 2, D_OUT]), ALU.add).then_inc(
                    x_summed, 1)

            def rstd_of(e, i):
                done = NEWTON_OPS * e
                if i == 0:
                    pool.wait_ge(aggr_done, e + 1)
                    wait(pool, x_normed, TILES * e)
                    wait(pool, newton, done)
                    pool.sem_inc(pool_joined, 1)
                    pool.tensor_scalar(var_eps[:, :], mean_var[:, :, 1], EPS, None, ALU.add).then_inc(newton, 1)
                    pool.wait_ge(newton, done + 1)
                    pool.sem_inc(pool_joined, 1)
                    pool.tensor_scalar(rstd.bitcast(INT32)[:, :], var_eps.bitcast(INT32)[:, :], -0.5,
                                       float(0x5f3759df), ALU.mult, ALU.add).then_inc(newton, 1)
                else:
                    done = done + 2 + 4 * (i - 1)
                    pool.wait_ge(newton, done)
                    pool.tensor_tensor(factor[:, :], rstd[:, :], rstd[:, :], ALU.mult).then_inc(newton, 1)
                    pool.wait_ge(newton, done + 1)
                    pool.tensor_tensor(factor[:, :], factor[:, :], var_eps[:, :], ALU.mult).then_inc(newton, 1)
                    pool.wait_ge(newton, done + 2)
                    pool.sem_inc(pool_joined, 1)
                    pool.tensor_scalar(factor[:, :], factor[:, :], -0.5, 1.5, ALU.mult, ALU.add).then_inc(newton, 1)
                    pool.wait_ge(newton, done + 3)
                    pool.tensor_tensor(rstd[:, :], rstd[:, :], factor[:, :], ALU.mult).then_inc(newton, 1)

            for i in range(NEWTON + 1):
                rstd_of(0, i)

            def load_adj(n, tile):
                i, c = n % ADJ_RING, n % CHUNKS
                pool.dma_start(adj_in[:, i:i + LOAD, :].rearrange("p a n -> p (a n)"),
                               adj[bass.ds(tile * P, P), c * CHUNK:(c + LOAD) * CHUNK]).then_inc(
                    adj_ready[i // LOAD], 16)

            for n in range(0, ADJ_RING, LOAD):
                load_adj(n, 0)
            for i in range(NEWTON + 1):
                rstd_of(1, i)
            pool.wait_ge(wide_in[1], WIDE_IN)
            for h in range(2):
                left_sum(0, h)

            def step(s, it):
                if POOL_MASKS <= s < STEPS:
                    parity, tile, c = chunk_of(s)
                    pool.wait_ge(risen, s + 1 + PERIOD * it)
                    half = scores[:, parity * TILES + tile, c * CHUNK + BANK:(c + 1) * CHUNK]
                    pool.tensor_tensor(half, half, mask[:, s % 2, BANK:CHUNK], ALU.add).then_inc(masked, 1)
                n = s - LOAD + 1 + ADJ_RING
                if n % LOAD == 0 and ADJ_RING <= n < STEPS:
                    pool.wait_ge(mask_done, s + 1 + PERIOD * it)
                    load_adj(n, n // CHUNKS + 2 * TILES * it)
                for i in range(2):
                    if e := x_due(s, X_SUM + i):
                        left_sum(e + 2 * it, i)
                for i in range(NEWTON + 1):
                    if e := x_due(s, X_RSTD[i]):
                        rstd_of(e + 2 * it, i)

            main(pool, step)

        @block.scalar
        def _(act):
            def turned_copy(q):
                for k in range(KT):
                    act.wait_ge(turned, KT * q + k + 1)
                    act.activation(rows_t[:, bass.ds(q, 1), k * GROUP:(k + 1) * GROUP].rearrange("p a n -> p (a n)"),
                                   pt[:, k], ACT.Copy).then_inc(turned_out, 1)

            def neigh_step(e, it):
                q = e + 2 * it
                par = e % 2
                if it_is(it, e, NEIGH_GROUPS - 2):
                    x_tanh(0, x_bank(0))
                if e < NEIGH_GROUPS - 1:
                    turned_copy(q + 1)
                act.wait_ge(first_done, q + 1)
                wait(act, hidden_lo, q - 1)
                act.activation(hidden[:, par], ps_hidden, ACT.Tanh, bias=b1[:, 0:1]).then_inc(hidden_done, 1)
                act.wait_ge(hidden_done, q + 1)
                wait(act, second_done, q - 1)
                act.activation(hidden_stack[:, par], hidden[:, par], ACT.Copy).then_inc(hidden_hi, 1)
                if it_is(it, e, 1):
                    act.wait_ge(consts_in[1], CONSTS_IN[1])
                    for k in range(KT):
                        x_turned_copy(0, k, ps[:, 1 - k, 0:BANK])

            def x_turned_copy(e, k, bank):
                act.wait_ge(x_turned, KT * e + k + 1)
                if k == 0:
                    wait(act, x_wide, e)
                act.activation(x_rows_t[:, k, :], bank, ACT.Relu).then_inc(x_turned_out, 1)

            def x_tanh(e, bank):
                act.wait_ge(x_first, e + 1)
                wait(act, agg_turned, e - 2)
                act.activation(agg[0:D_HID, :], bank[0:D_HID, :], ACT.Tanh, bias=b1[0:D_HID, 1:2]).then_inc(x_hidden, 1)

            turned_copy(0)
            act.wait_ge(consts_in[0], CONSTS_IN[0])
            encode(act, neigh_step)

            def hi(s, u, it):
                b = s - BACK_LAG
                if not 0 <= b < STEPS:
                    return
                j = 2 * b + u + 2 * PERIOD * it
                act.wait_ge(block_turned, j + 1)
                if b == 0:
                    act.wait_ge(second_done, NEIGH_GROUPS)
                if 2 * b + u >= HI_RING:
                    act.wait_ge(block_used, j - HI_RING + 1)
                act.activation(pt_hi[:, (2 * b + u) % HI_RING], pt[:, u], ACT.Copy).then_inc(hi_done, 1)

            def step(s, it):
                k = s + PERIOD * it
                hi(s, 0, it)
                b = s - COPY_LAG
                if b >= 0 and b % GSTEPS == 0 and b // GSTEPS < GROUPS:
                    g = b // GSTEPS + 2 * it
                    act.wait_ge(block_used, (g + 1) * BLOCKS)
                    wait(act, agg_turned, g)
                    act.wait_ge(x_second, min(GROUPS, g + 3) if isinstance(g, int) else g + 3)
                    act.activation(agg[:, :], pa[:, b // GSTEPS % 2], ACT.Copy).then_inc(agg_out, 1)
                if s < STEPS:
                    parity, tile, c = chunk_of(s)
                    act.wait_ge(scored, k + 1)
                    if s == GSTEPS:
                        act.wait_ge(second_done, NEIGH_GROUPS)
                    if s == GSTEPS + CHUNKS:
                        act.wait_ge(v_lo_done, NEIGH_GROUPS)
                    if tile == 0 and s >= 2 * GSTEPS:
                        act.wait_ge(block_turned, (s // GSTEPS - 2 + 2 * it) * BLOCKS + (c + 1) * BLOCKS // CHUNKS)
                    act.activation(scores[:, parity * TILES + tile, c * CHUNK:(c + 1) * CHUNK], ps[:, s % 2],
                                   ACT.Relu, scale=RISE).then_inc(risen, 1)
                hi(s, 1, it)
                e = s - EXP_LAG
                if 0 <= e < STEPS:
                    parity, tile, c = chunk_of(e)
                    t = e // CHUNKS + 2 * TILES * it
                    if c == 0:
                        act.wait_ge(top_done, t + 1)
                        if tile == 0 and e >= 2 * GSTEPS:
                            act.wait_ge(sums_done, e // GSTEPS - 1 + 2 * it)
                    cols = scores[:, parity * TILES + tile, c * CHUNK:(c + 1) * CHUNK]
                    act.activation(cols, cols, ACT.Exp, bias=neg_top[:, tile % 2, :],
                                   accum_out=sums[:, parity, tile, c:c + 1]).then_inc(exp_done, 1)
                if value_due(s - 1) is not None:
                    v = value_due(s - 1)
                    act.wait_ge(wide_done, v + 1)
                    act.activation(v_halves(v, v_hi), ps_value[:, v % 2], ACT.Copy).then_inc(v_hi_done, 1)
                for k in range(KT):
                    if e := x_due(s, X_TURN + k):
                        x_turned_copy(e + 2 * it, k, x_bank(e))
                if e := x_due(s, X_TANH):
                    x_tanh(e + 2 * it, x_bank(e))

            main(act, step)

        @block.vector
        def _(dve):
            def x_stats(e, i, rows_of_x=x_rows):
                if rows_of_x is x_rows:
                    dve.wait_ge(x_rows_in, 16 * (e + 1))
                else:
                    dve.wait_ge(x_ahead_in, 16)
                wait(dve, aggr_done, e)
                dve.bn_stats(stats[:, i, :], rows_of_x[:, i, :]).then_inc(stats_done, 1)

            def x_aggr(e):
                dve.wait_ge(stats_done, TILES * (e + 1))
                wait(dve, x_normed, TILES * e)
                wait(dve, newton, NEWTON_OPS * e)
                dve.sem_inc(joined, 1)
                for i in range(TILES):
                    last = dve.bn_aggr(mean_var[:, i, :], stats[:, i, :])
                last.then_inc(aggr_done, 1)

            def att_high(par, q):
                dve.wait_ge(second_done, q + 1)
                dve.tensor_scalar(neib[:, bass.ds(q * GROUP, GROUP)], ps_att[par], b2[:, 0:1], None,
                                  ALU.add).then_inc(att_hi, 1)

            def att_low(par, q):
                dve.wait_ge(att_hi, q + 1)
                for p in (D_HID, 3 * D_HID):
                    part = neib[p:p + D_HID, bass.ds(q * GROUP, GROUP)]
                    last = dve.scalar_tensor_tensor(part, ps_att[par][p:p + D_HID, :], b2[p:p + D_HID, 0:1],
                                                    part.bitcast(FP32), ALU.add, ALU.subtract)
                last.then_inc(att_out, 1)

            def neigh_step(e, it):
                q = e + 2 * it
                par = e % 2
                if it_is(it, e, 1):
                    for i in range(TILES):
                        x_normalise(0, i)
                    x_aggr(1)
                if it_is(it, e, NEIGH_GROUPS - 1):
                    x_stack_high(0, 0, x_bank(0))
                    x_stack_low(0, 0, x_bank(0))
                    mask_of(0, 0)
                first = it_is(it, e, 0)
                if not first:
                    att_high(1 - par, q - 1)
                dve.wait_ge(hidden_hi, q + 1)
                low = hidden_stack[P // 2:P, par]
                dve.tensor_tensor(low, hidden[P // 2:P, par], low.bitcast(FP32), ALU.subtract).then_inc(hidden_lo, 1)
                if not first:
                    att_low(1 - par, q - 1)

            def x_normalise(e, i):
                dve.wait_ge(x_rows_in, 16 * (e + 1))
                dve.wait_ge(newton, NEWTON_OPS * (e + 1))
                dve.tensor_scalar(x_rows[:, i, :], x_rows[:, i, :], mean_var[:, i, 0:1],
                                  rstd[:, i:i + 1], ALU.subtract, ALU.mult).then_inc(x_normed, 1)

            def x_stack_high(e, par, bank):
                dve.wait_ge(x_second, e + 1)
                wait(dve, scored, GSTEPS * (e - 1))
                dve.tensor_scalar(xs[:, par, :], bank, b2[:, 1:2], None, ALU.add).then_inc(x_att_hi, 1)

            def x_stack_low(e, par, bank):
                dve.wait_ge(x_att_hi, e + 1)
                low = xs[P // 2:P, par, :]
                dve.scalar_tensor_tensor(low, bank[P // 2:P, :], b2[P // 2:P, 1:2], low.bitcast(FP32),
                                         ALU.add, ALU.subtract).then_inc(x_att, 1)

            def x_left_out(e, bank):
                dve.wait_ge(x_summed, 2 * (e + 1))
                dve.wait_ge(x_wide, e + 1)
                dve.tensor_tensor(x_left[:, :], bank, x_left[:, :], ALU.add).then_inc(left_done, 1)

            def value_low(v):
                dve.wait_ge(v_hi_done, v + 1)
                dve.tensor_tensor(v_halves(v, v_lo), ps_value[:, v % 2], v_halves(v, v_hi).bitcast(FP32),
                                  ALU.subtract).then_inc(v_lo_done, 1)

            for i in range(TILES):
                x_stats(0, i)
            x_aggr(0)
            dve.wait_ge(consts_in[0], CONSTS_IN[0])
            w2_wide = w2_stack.rearrange("p (c h) -> p c h", h=D_HID)
            w2_copies = w2_n.rearrange("p (c h) -> p c h", c=1).to_broadcast([P, P // D_HID, D_HID])
            dve.tensor_copy(w2_wide, w2_copies).then_inc(w2_hi, 1)
            dve.wait_ge(w2_hi, 1)
            for p in (D_HID, 3 * D_HID):
                part = w2_wide[p:p + D_HID]
                last = dve.tensor_tensor(part, w2_copies[p:p + D_HID], part.bitcast(FP32), ALU.subtract)
            last.then_inc(w2_done, 1)
            for i in range(TILES):
                x_stats(1, i, x_ahead)
            dve.wait_ge(b2_in, B2_IN)

            def mask_of(n, it):
                k = n + PERIOD * it
                dve.wait_ge(adj_ready[n % ADJ_RING // LOAD], 16 * (n // ADJ_RING + 1) + 16 * PERIOD // ADJ_RING * it)
                if n >= 2:
                    dve.wait_ge(scored, k - 1)
                if n - 2 >= POOL_MASKS:
                    dve.wait_ge(masked, k - 1 - POOL_MASKS)
                dve.tensor_scalar(mask[:, n % 2, :], adj_in[:, n % ADJ_RING, :], 0.0, MASKED, ALU.is_le,
                                  ALU.mult).then_inc(mask_done, 1)

            def lo(s, u, it):
                b = s - BACK_LAG
                if not 0 <= b < STEPS:
                    return
                j = 2 * b + u + 2 * PERIOD * it
                dve.wait_ge(hi_done, j + 1)
                if b == 0:
                    dve.wait_ge(second_done, NEIGH_GROUPS)
                if 2 * b + u >= 2:
                    dve.wait_ge(block_used, j - 1)
                dve.tensor_tensor(pt_lo[:, u], pt[:, u], pt_hi[:, (2 * b + u) % HI_RING].bitcast(FP32),
                                  ALU.subtract).then_inc(lo_done, 1)

            def step(s, it):
                if s < POOL_MASKS:
                    mask_of(s + 1, it)
                n = s - 1
                if 0 <= n < STEPS:
                    parity, tile, c = chunk_of(n)
                    k = n + PERIOD * it
                    cols = scores[:, parity * TILES + tile, c * CHUNK:(c + 1) * CHUNK]
                    dve.wait_ge(risen, k + 1)
                    if n >= POOL_MASKS:
                        dve.wait_ge(masked, k + 1 - POOL_MASKS)
                    if c:
                        dve.wait_ge(leaked, k)
                    start = top[:, tile % 2, c - 1:c] if c else -3.0e38
                    if c == 0 and n >= 2 * CHUNKS:
                        dve.wait_ge(top_done, n // CHUNKS - 1 + 2 * TILES * it)
                    dve.sem_inc(joined, 1)
                    dve.tensor_tensor_reduce(cols, ps[:, n % 2], cols, SLOPE, start, ALU.add, ALU.max,
                                             top[:, tile % 2, c:c + 1]).then_inc(leaked, 1)
                lo(s, 0, it)
                if POOL_MASKS <= s < STEPS - 1:
                    mask_of(s + 1, it)
                if value_due(s - 2) is not None:
                    value_low(value_due(s - 2))
                if s == 1:
                    att_high(1, NEIGH_GROUPS - 1)
                    att_low(1, NEIGH_GROUPS - 1)
                lo(s, 1, it)
                if 0 <= n < STEPS and n % CHUNKS == CHUNKS - 1:
                    dve.wait_ge(leaked, n + 1 + PERIOD * it)
                    if n >= 2 * CHUNKS:
                        dve.wait_ge(exp_done, (n // CHUNKS - 1) * CHUNKS + PERIOD * it)
                    dve.tensor_scalar(neg_top[:, n // CHUNKS % 2, :], top[:, n // CHUNKS % 2, CHUNKS - 1:CHUNKS],
                                      -1.0, None, ALU.mult).then_inc(top_done, 1)
                for i in range(TILES):
                    if e := x_due(s, X_STATS + i):
                        x_stats(e + 2 * it, i)
                    if e := x_due(s, X_NORM[i]):
                        x_normalise(e + 2 * it, i)
                if e := x_due(s, X_AGGR):
                    x_aggr(e + 2 * it)
                if e := x_due(s, X_STACK):
                    x_stack_high(e + 2 * it, e % 2, x_bank(e))
                if e := x_due(s, X_STACK + 1):
                    x_stack_low(e + 2 * it, e % 2, x_bank(e))
                if s == 1:
                    x_left_out(0, pa[:, 0, :])
                if e := x_due(s, X_LEFT):
                    x_left_out(e + 2 * it, x_bank(e))
                b = s - SUM_LAG
                if b >= 0 and b % GSTEPS == 0 and b // GSTEPS < GROUPS:
                    g = b // GSTEPS + 2 * it
                    parity = b // GSTEPS % 2
                    dve.wait_ge(exp_done, (g + 1) * GSTEPS)
                    if b:
                        dve.wait_ge(sums_done, g)
                    dve.reduce_sum(row_sum[:, :], sums[:, parity], axis=AX.X).then_inc(row_sum_done, 1)
                    dve.wait_ge(row_sum_done, g + 1)
                    if b:
                        dve.wait_ge(right_done, g)
                    dve.reciprocal(inv_sum[:, parity, :], row_sum[:, :]).then_inc(sums_done, 1)
                b = s - FIN_LAG
                if b >= 0 and b % GSTEPS < 2 and b // GSTEPS < GROUPS:
                    g = b // GSTEPS + 2 * it
                    parity = b // GSTEPS % 2
                    if b % GSTEPS == 0:
                        dve.wait_ge(agg_turned, g + 1)
                        dve.wait_ge(sums_done, g + 1)
                        dve.wait_ge(x_right_in, 16 * (g + 1))
                    for i in range(b % GSTEPS * TILES // 2, (b % GSTEPS + 1) * TILES // 2):
                        last = dve.scalar_tensor_tensor(
                            x_right[:, i, :], pa[:, parity, i * P:(i + 1) * P], inv_sum[:, parity, i:i + 1],
                            x_right[:, i, :], ALU.mult, ALU.add)
                    if b % GSTEPS == 1:
                        last.then_inc(right_done, 1)

            encode(dve, neigh_step)
            main(dve, step)

        @block.tensor
        def _(pe):
            def turn_rows(q, e, it):
                par = e % 2
                pe.wait_ge(rows_in[par], 16 * (e // 2 + it + 1))
                for k in range(KT):
                    wait(pe, turned_out, KT * (q - 1) + k + 1)
                    for i in range(TILES):
                        last = pe.transpose(pt[:, k, i * P:(i + 1) * P], rows[:, par, i, k * P:(k + 1) * P],
                                            ident[:, :])
                    last.then_inc(turned, 1)

            def second_layer(par, q):
                pe.wait_ge(hidden_lo, q + 1)
                wait(pe, att_out, q - 1)
                pe.matmul(ps_att[par], w2_stack, hidden_stack[:, par], start=True, stop=True).then_inc(second_done, 1)

            def neigh_step(e, it):
                q = e + 2 * it
                par = e % 2
                if it_is(it, e, NEIGH_GROUPS - 2):
                    for i in range(2 * KT):
                        x_first_layer(0, i, x_bank(0))
                if e < NEIGH_GROUPS - 1:
                    turn_rows(q + 1, e + 1, it)
                pe.wait_ge(turned_out, KT * (q + 1))
                wait(pe, hidden_done, q)
                for k in range(KT):
                    last = pe.matmul(ps_hidden, w1_n[:, k, :],
                                     rows_t[:, bass.ds(q, 1), k * GROUP:(k + 1) * GROUP].rearrange("p a n -> p (a n)"),
                                     start=k == 0, stop=k == KT - 1)
                last.then_inc(first_done, 1)
                if it_is(it, e, 1):
                    pe.wait_ge(w2_done, 1)
                if not it_is(it, e, 0):
                    second_layer(1 - par, q - 1)
                if it_is(it, e, 1):
                    pe.wait_ge(consts_in[1], CONSTS_IN[1])
                    for k in range(KT):
                        x_turn(0, k, ps[:, 1 - k, 0:BANK])
                if it_is(it, e, NEIGH_GROUPS - 2):
                    for h in range(2):
                        x_second_layer(0, h, x_bank(0))

            def value_layer(v, h):
                if h == 0:
                    if v == 0:
                        pe.wait_ge(wide_in[0], WIDE_IN)
                    if v < 2:
                        pe.wait_ge(turned_out, KT * NEIGH_GROUPS)
                    else:
                        pe.wait_ge(v_lo_done, v - 1)
                for i in range(h * TILES // 2, (h + 1) * TILES // 2):
                    for k in range(KT):
                        last = pe.matmul(ps_value[:, v % 2, i * D_OUT:(i + 1) * D_OUT],
                                         rows_t[:, v, k * GROUP + i * P:k * GROUP + (i + 1) * P],
                                         w_v[:, k, :], start=k == 0, stop=False)
                    last = pe.matmul(ps_value[:, v % 2, i * D_OUT:(i + 1) * D_OUT], ones[:, :], b_v[0:1, 0, :],
                                     start=False, stop=True)
                if h == 1:
                    last.then_inc(wide_done, 1)

            def x_turn(e, k, bank):
                if k == 0:
                    wait(pe, left_done, min(e, 1) if isinstance(e, int) else e)
                    pe.wait_ge(x_normed, TILES * (e + 1))
                    wait(pe, right_done, e - 2)
                elif not isinstance(e, int) or e:
                    pe.wait_ge(x_turned_out, KT * e + k)
                for i in range(TILES):
                    last = pe.transpose(bank[:, i * P:(i + 1) * P], x_rows[:, i, k * P:(k + 1) * P], ident[:, :])
                last.then_inc(x_turned, 1)

            def x_first_layer(e, i, bank):
                h, k = i // KT, i % KT
                half = slice(h * BANK // 2, (h + 1) * BANK // 2)
                pe.wait_ge(x_turned_out, KT * (e + 1))
                last = pe.matmul(bank[0:D_HID, half], w1_x[:, k, :], x_rows_t[:, k, half],
                                 start=k == 0, stop=k == KT - 1)
                if i == 2 * KT - 1:
                    last.then_inc(x_first, 1)

            def x_second_layer(e, h, bank):
                half = slice(h * BANK // 2, (h + 1) * BANK // 2)
                pe.wait_ge(x_hidden, e + 1)
                last = pe.matmul(bank[:, half], w2_x[:, :], agg[0:D_HID, half], start=True, stop=True)
                if h:
                    last.then_inc(x_second, 1)

            def x_wide_layer(e, tiles, bank):
                pe.wait_ge(x_att, e + 1)
                for i in tiles:
                    for k in range(KT):
                        last = pe.matmul(bank[:, i * D_OUT:(i + 1) * D_OUT], x_rows_t[:, k, i * P:(i + 1) * P],
                                         w_fx[:, k, :], start=k == 0, stop=k == KT - 1)
                if i == TILES - 1:
                    last.then_inc(x_wide, 1)

            pe.wait_ge(made, 3)
            for _ in range(WARM_UP):
                pe.transpose(pa[:, 1, 0:P], ident[:, :], ident[:, :])
            turn_rows(0, 0, 0)
            pe.wait_ge(consts_in[0], CONSTS_IN[0])
            encode(pe, neigh_step)

            def score(s, h, it):
                if s >= STEPS:
                    return
                k = s + PERIOD * it
                parity, tile, c = chunk_of(s)
                if h == 0:
                    pe.wait_ge(mask_done, k + 1)
                    if s >= 2:
                        pe.wait_ge(leaked, k - 1)
                    if s < CHUNKS:
                        pe.wait_ge(att_out, NEIGH_GROUPS - 1 if s == 1 else (s + 1) * CHUNK // GROUP)
                    if tile == 0 and c == 0:
                        pe.wait_ge(x_att, s // GSTEPS + 2 * it + 1)
                half = slice(h * BANK, (h + 1) * BANK)
                on_pool = h == 1 and s >= POOL_MASKS
                if not on_pool:
                    pe.matmul(ps[:, s % 2, half], ident_bf16[:, :], mask[:, s % 2, half], start=True, stop=False)
                last = pe.matmul(ps[:, s % 2, half], xs[:, parity, tile * P:(tile + 1) * P],
                                 neib[:, c * CHUNK + h * BANK:c * CHUNK + (h + 1) * BANK], start=on_pool, stop=True)
                if h == 1:
                    last.then_inc(scored, 1)

            def turn(s, u, it):
                b = s - BACK_LAG
                if not 0 <= b < STEPS:
                    return
                parity = b // GSTEPS % 2
                n = 2 * (b % GSTEPS) + u
                j = 2 * b + u + 2 * PERIOD * it
                per_chunk = BLOCKS // CHUNKS
                if n % per_chunk == 0:
                    pe.wait_ge(exp_done, (b // GSTEPS + 1) * GSTEPS - CHUNKS + n // per_chunk + 1 + PERIOD * it)
                if b == 0 and u == 0:
                    pe.wait_ge(v_lo_done, NEIGH_GROUPS)
                if 2 * b + u >= 2:
                    pe.wait_ge(lo_done, j - 1)
                for i in range(TILES):
                    last = pe.transpose(pt[:, u, i * P:(i + 1) * P],
                                        scores[:, parity * TILES + i, n * P:(n + 1) * P], ident[:, :])
                last.then_inc(block_turned, 1)

            def product(s, u, it):
                b2_ = 2 * (s - BACK_LAG) + u
                if not 0 <= b2_ < 2 * STEPS:
                    return
                j = b2_ + 2 * PERIOD * it
                n = b2_ % BLOCKS
                parity = b2_ // BLOCKS % 2
                pe.wait_ge(lo_done, j + 1)
                if n == 0:
                    g = b2_ // BLOCKS + 2 * it
                    wait(pe, right_done, g - 1)
                    pe.wait_ge(left_done, min(GROUPS, g + 2) if isinstance(g, int) else g + 2)
                acc = pa[:, parity, :]
                pe.matmul(acc, v_hi[:, n, :], pt_hi[:, b2_ % HI_RING, :], start=n == 0, stop=False)
                pe.matmul(acc, v_lo[:, n, :], pt_hi[:, b2_ % HI_RING, :], start=False, stop=False)
                pe.matmul(acc, v_hi[:, n, :], pt_lo[:, b2_ % 2, :], start=False, stop=n == BLOCKS - 1).then_inc(
                    block_used, 1)

            def step(s, it):
                turn(s, 0, it)
                score(s, 0, it)
                score(s, 1, it)
                product(s, -2, it)
                turn(s, 1, it)
                product(s, -1, it)
                b = s - FIN_LAG
                if b >= 0 and b % GSTEPS == 0 and b // GSTEPS < GROUPS:
                    g = b // GSTEPS + 2 * it
                    pe.wait_ge(agg_out, g + 1)
                    for i in range(TILES):
                        last = pe.transpose(pa[:, b // GSTEPS % 2, i * P:(i + 1) * P], agg[:, i * P:(i + 1) * P],
                                            ident[:, :])
                    last.then_inc(agg_turned, 1)
                if s == 0:
                    second_layer(1, NEIGH_GROUPS - 1)
                    pe.wait_ge(hidden_done, NEIGH_GROUPS)
                    pe.wait_ge(wide_in[1], WIDE_IN)
                    x_wide_layer(0, range(TILES), pa[:, 0, :])
                for i in range(2):
                    if e := x_due(s, X_TURN + i):
                        x_turn(e + 2 * it, i, x_bank(e))
                    if e := x_due(s, X_SECOND + i):
                        x_second_layer(e + 2 * it, i, x_bank(e))
                for i in range(2 * KT):
                    if e := x_due(s, X_FIRST + i):
                        x_first_layer(e + 2 * it, i, x_bank(e))
                for i in range(TILES):
                    if e := x_due(s, X_WIDE + i):
                        x_wide_layer(e + 2 * it, [i], x_bank(e))
                for h in range(2):
                    if value_due(s - h) is not None:
                        value_layer(value_due(s - h), h)

            main(pe, step)


INPUTS = ["x", "adj", "L0_gnn_neigh", "L0_gnn_Wx1", "L0_gnn_bx1", "L0_gnn_Wx2", "L0_gnn_bx2", "L0_gnn_Wn1",
          "L0_gnn_bn1", "L0_gnn_Wn2", "L0_gnn_bn2", "L0_gnn_Wv", "L0_gnn_bv", "L0_gnn_Wfx", "L0_gnn_bfx"]


def kernel(**inputs):
    import numpy as np
    import concourse.bacc as bacc
    from concourse.bass_utils import run_bass_kernel_spmd

    nc = bacc.Bacc("TRN2", target_bir_lowering=False, num_devices=1, dynamic_dma_scratch_size=DMA_RING)
    arrays, args = {}, []
    for name in INPUTS:
        a = np.ascontiguousarray(inputs[name])
        arrays[f"in_{name}"] = a
        args.append(nc.dram_tensor(f"in_{name}", a.shape, mybir.dt.from_np(a.dtype), kind="ExternalInput").ap())
    out = nc.dram_tensor("out_h", (N_X, 2 * D_OUT), FP32, kind="ExternalOutput").ap()
    build(nc, *args, out)
    return run_bass_kernel_spmd(nc, [arrays], core_ids=[0]).results[0]["out_h"]
```
